# Optimizing a Trainium2 kernel written in Bass

```python
import numpy as np
import jax
import jax.numpy as jnp

def _softmax(x, axis=-1):
    return jax.nn.softmax(x, axis=axis)

def _gelu(x):
    return jax.nn.gelu(x, approximate=True)

def _silu(x):
    return jax.nn.silu(x)

def _sigmoid(x):
    return jax.nn.sigmoid(x)

def _layernorm(x, axis=-1, eps=1e-05):
    m = jnp.mean(x, axis=axis, keepdims=True)
    v = jnp.var(x, axis=axis, keepdims=True)
    return (x - m) / jnp.sqrt(v + eps)

def _scatter_add(tgt, idx, src, axis=0):
    return tgt.at[idx].add(src)

def _segment_sum(src, seg, n):
    return jax.ops.segment_sum(src, seg, n)
kernel_name = 'mk_decoder_preln_d1_seqx_r4_30eed7'

def setup_inputs(seed: int=0):
    np.random.seed(seed)
    _w = jnp.asarray

    def _rec_inputs():
        import jax
        import jax.numpy as jnp
        _rk = jax.random.key(seed)
        x = 7.22e-05 + 1 * jax.random.normal(jax.random.fold_in(_rk, 1), (8, 256, 256), jnp.float32)
        _lenS = 256 - jax.random.randint(jax.random.fold_in(_rk, 7), (8,), 0, max(1, 256 // 4) + 1, jnp.int32)
        _lenS2 = 256 - jax.random.randint(jax.random.fold_in(_rk, 8), (8,), 0, max(1, 256 // 4) + 1, jnp.int32)
        _ctx_1024P = jax.random.normal(jax.random.fold_in(_rk, 11), (8, 16, 256), jnp.float32)
        _ctx_1024c = jax.random.dirichlet(jax.random.fold_in(_rk, 511), 0.3 * jnp.ones((16,), jnp.float32), (8, 256))
        _ctx_1024t = jnp.einsum('bsk,bkd->bsd', _ctx_1024c, _ctx_1024P)
        _ctx_1024t = _ctx_1024t * jax.lax.rsqrt(jnp.mean(jnp.square(_ctx_1024t)) + 1e-12) * 0.953939
        ctx_1024 = 4.13588e-05 + 0.999923 * (_ctx_1024t + 0.3 * jax.random.normal(jax.random.fold_in(_rk, 611), (8, 256, 256), jnp.float32))
        return (x, ctx_1024)
    x, ctx_1024 = _rec_inputs()

    def _L0_attn_setup():
        import jax, jax.numpy as jnp
        import numpy as np
        D_MODEL, D_HIDDEN = (256, 512)
        B, L = (4, 1024)

        def _lin(x, w, b=None):
            y = jnp.einsum('bld,od->blo', x, w)
            return y if b is None else y + b

        def _depthwise_conv(x, conv_w, conv_b):
            lhs = jnp.transpose(x, (0, 2, 1))
            y = jax.lax.conv_general_dilated(lhs, conv_w, window_strides=(1,), padding=[(1, 1)], dimension_numbers=('NCH', 'OIH', 'NCH'), feature_group_count=D_MODEL)
            y = y + conv_b[None, :, None]
            return jnp.transpose(y, (0, 2, 1))
        key = jax.random.key(seed)
        ks = jax.random.split(key, 16)
        r = lambda k, shape, s: s * jax.random.normal(k, shape, dtype=jnp.float32)
        inp = {'x': r(ks[0], (B, L, D_MODEL), 1.0), 'w1': r(ks[1], (D_MODEL, D_MODEL), 0.02), 'w2': r(ks[2], (D_MODEL, D_MODEL), 0.02), 'w3': r(ks[3], (D_MODEL, D_MODEL), 0.02), 'conv_w': r(ks[4], (D_MODEL, 1, 3), 0.1), 'conv_b': r(ks[5], (D_MODEL,), 0.02), 'A_w': r(ks[6], (D_HIDDEN, D_MODEL), 0.001), 'A_b': jnp.ones((D_HIDDEN,), jnp.float32), 'B_w': r(ks[7], (D_HIDDEN, D_MODEL), 0.02), 'B_b': jnp.zeros((D_HIDDEN,), jnp.float32), 'C_w': r(ks[8], (D_MODEL, D_HIDDEN), 0.02), 'C_b': jnp.zeros((D_MODEL,), jnp.float32), 'D_w': r(ks[9], (D_MODEL, D_MODEL), 0.02), 'D_b': jnp.zeros((D_MODEL,), jnp.float32), 'dl_w': r(ks[10], (D_HIDDEN, D_MODEL), 0.001), 'dl_b': -5.0 * jnp.ones((D_HIDDEN,), jnp.float32)}
        return inp
    _L0_attn_all = _L0_attn_setup()
    _L0_attn_in = {k: v for k, v in _L0_attn_all.items() if k in ('w1', 'w2', 'w3', 'conv_w', 'conv_b', 'A_w', 'A_b', 'B_w', 'B_b', 'C_w', 'C_b', 'D_w', 'D_b', 'dl_w', 'dl_b')}
    del _L0_attn_all

    def _L0_xattn_setup():
        import jax, jax.numpy as jnp
        import numpy as np
        EMB = 256
        HEADS = 16
        HEAD_DIM = EMB // HEADS
        SCALE = 1.0 / np.sqrt(HEAD_DIM)
        key = jax.random.key(seed)
        ks = jax.random.split(key, 11)
        B, L, E = (4, 512, EMB)
        s = 1.0 / np.sqrt(E)
        inp = {'Q': jax.random.normal(ks[0], (B, L, E), jnp.float32), 'K': jax.random.normal(ks[1], (B, L, E), jnp.float32), 'V': jax.random.normal(ks[2], (B, L, E), jnp.float32), 'WQ': jax.random.normal(ks[3], (E, E), jnp.float32) * s, 'bQ': jax.random.normal(ks[4], (E,), jnp.float32) * s, 'WK': jax.random.normal(ks[5], (E, E), jnp.float32) * s, 'bK': jax.random.normal(ks[6], (E,), jnp.float32) * s, 'WV': jax.random.normal(ks[7], (E, E), jnp.float32) * s, 'bV': jax.random.normal(ks[8], (E,), jnp.float32) * s, 'WO': jax.random.normal(ks[9], (E, E), jnp.float32) * s, 'bO': jax.random.normal(ks[10], (E,), jnp.float32) * s}
        return inp
    _L0_xattn_all = _L0_xattn_setup()
    _L0_xattn_in = {k: v for k, v in _L0_xattn_all.items() if k in ('WQ', 'bQ', 'WK', 'bK', 'WV', 'bV', 'WO', 'bO')}
    del _L0_xattn_all

    def _L0_ffn_setup():
        import jax, jax.numpy as jnp
        import numpy as np
        NUM_EXPERTS = 8
        TOP_K = 2
        CAP_RATIO = 1.25
        INIT_STD = 0.02
        key = jax.random.key(seed)
        k1, k2, k3, k4 = jax.random.split(key, 4)
        B, T, H, F = (4, 512, 256, 1024)
        x = jax.random.normal(k1, (B, T, H), jnp.float32)
        router_w = jax.random.normal(k2, (NUM_EXPERTS, H), jnp.float32) * INIT_STD
        w1 = jax.random.normal(k3, (NUM_EXPERTS, H, F), jnp.float32) * INIT_STD
        w2 = jax.random.normal(k4, (NUM_EXPERTS, F, H), jnp.float32) * INIT_STD
        return {'x': x, 'router_w': router_w, 'w1': w1, 'w2': w2}
    _L0_ffn_all = _L0_ffn_setup()
    _L0_ffn_in = {k: v for k, v in _L0_ffn_all.items() if k in ('router_w', 'w1', 'w2')}
    del _L0_ffn_all
    return {'x': x, 'ctx_1024': ctx_1024, 'L0_attn_w1': _L0_attn_in['w1'], 'L0_attn_w2': _L0_attn_in['w2'], 'L0_attn_w3': _L0_attn_in['w3'], 'L0_attn_conv_w': _L0_attn_in['conv_w'], 'L0_attn_conv_b': _L0_attn_in['conv_b'], 'L0_attn_A_w': _L0_attn_in['A_w'], 'L0_attn_A_b': _L0_attn_in['A_b'], 'L0_attn_B_w': _L0_attn_in['B_w'], 'L0_attn_B_b': _L0_attn_in['B_b'], 'L0_attn_C_w': _L0_attn_in['C_w'], 'L0_attn_C_b': _L0_attn_in['C_b'], 'L0_attn_D_w': _L0_attn_in['D_w'], 'L0_attn_D_b': _L0_attn_in['D_b'], 'L0_attn_dl_w': _L0_attn_in['dl_w'], 'L0_attn_dl_b': _L0_attn_in['dl_b'], 'L0_xattn_WQ': _L0_xattn_in['WQ'], 'L0_xattn_bQ': _L0_xattn_in['bQ'], 'L0_xattn_WK': _L0_xattn_in['WK'], 'L0_xattn_bK': _L0_xattn_in['bK'], 'L0_xattn_WV': _L0_xattn_in['WV'], 'L0_xattn_bV': _L0_xattn_in['bV'], 'L0_xattn_WO': _L0_xattn_in['WO'], 'L0_xattn_bO': _L0_xattn_in['bO'], 'L0_ffn_router_w': _L0_ffn_in['router_w'], 'L0_ffn_w1': _L0_ffn_in['w1'], 'L0_ffn_w2': _L0_ffn_in['w2']}

def reference(x, ctx_1024, L0_attn_w1, L0_attn_w2, L0_attn_w3, L0_attn_conv_w, L0_attn_conv_b, L0_attn_A_w, L0_attn_A_b, L0_attn_B_w, L0_attn_B_b, L0_attn_C_w, L0_attn_C_b, L0_attn_D_w, L0_attn_D_b, L0_attn_dl_w, L0_attn_dl_b, L0_xattn_WQ, L0_xattn_bQ, L0_xattn_WK, L0_xattn_bK, L0_xattn_WV, L0_xattn_bV, L0_xattn_WO, L0_xattn_bO, L0_ffn_router_w, L0_ffn_w1, L0_ffn_w2):
    import jax
    import jax.numpy as jnp

    def _L0_attn_ref(x, w1, w2, w3, conv_w, conv_b, A_w, A_b, B_w, B_b, C_w, C_b, D_w, D_b, dl_w, dl_b):
        import jax, jax.numpy as jnp
        import numpy as np
        D_MODEL, D_HIDDEN = (256, 512)
        B, L = (4, 1024)

        def _lin(x, w, b=None):
            y = jnp.einsum('bld,od->blo', x, w)
            return y if b is None else y + b

        def _depthwise_conv(x, conv_w, conv_b):
            lhs = jnp.transpose(x, (0, 2, 1))
            y = jax.lax.conv_general_dilated(lhs, conv_w, window_strides=(1,), padding=[(1, 1)], dimension_numbers=('NCH', 'OIH', 'NCH'), feature_group_count=D_MODEL)
            y = y + conv_b[None, :, None]
            return jnp.transpose(y, (0, 2, 1))
        x = _lin(x, w1)
        x = _depthwise_conv(x, conv_w, conv_b)
        x = jax.nn.silu(x)
        x_delta = jax.nn.softplus(_lin(x, dl_w, dl_b))
        A_t = _lin(x, A_w, A_b)
        A_bar = jnp.exp(-x_delta * A_t)
        B_x = _lin(x, B_w, B_b)
        A_cum = jnp.cumprod(A_bar, axis=1)
        h = jnp.cumsum(B_x * A_cum, axis=1)
        ssm_out = _lin(h, C_w, C_b) + _lin(x, D_w, D_b)
        x_res = jax.nn.silu(_lin(ssm_out, w2))
        z = ssm_out * x_res
        out = ssm_out + _lin(z, w3)
        return out

    def _L0_xattn_ref(Q, K, V, WQ, bQ, WK, bK, WV, bV, WO, bO):
        import jax, jax.numpy as jnp
        import numpy as np
        EMB = 256
        HEADS = 16
        HEAD_DIM = EMB // HEADS
        SCALE = 1.0 / np.sqrt(HEAD_DIM)
        B, L, E = Q.shape
        q = Q @ WQ + bQ
        k = K @ WK + bK
        v = V @ WV + bV
        q = q.reshape(B, L, HEADS, HEAD_DIM).transpose(0, 2, 1, 3)
        k = k.reshape(B, L, HEADS, HEAD_DIM).transpose(0, 2, 1, 3)
        v = v.reshape(B, L, HEADS, HEAD_DIM).transpose(0, 2, 1, 3)
        scores = jnp.einsum('bhqd,bhkd->bhqk', q, k) * SCALE
        causal = jnp.tril(jnp.ones((L, L), dtype=bool))
        scores = jnp.where(causal, scores, -jnp.inf)
        probs = jax.nn.softmax(scores, axis=-1)
        out = jnp.einsum('bhqk,bhkd->bhqd', probs, v)
        out = out.transpose(0, 2, 1, 3).reshape(B, L, E)
        return out @ WO + bO

    def _L0_ffn_ref(x, router_w, w1, w2):
        import jax, jax.numpy as jnp
        import numpy as np
        NUM_EXPERTS = 8
        TOP_K = 2
        CAP_RATIO = 1.25
        INIT_STD = 0.02
        B, T, H = x.shape
        E, K = (NUM_EXPERTS, TOP_K)
        xf = x.reshape(-1, H)
        N = xf.shape[0]
        P = N * K
        capacity = int(CAP_RATio * N * K / E) + 1 if False else int(CAP_RATIO * N * K / E) + 1
        logits = xf @ router_w.T
        probs = jax.nn.softmax(logits, axis=-1)
        k_probs, k_idx = jax.lax.top_k(probs, K)
        k_probs = k_probs / jnp.sum(k_probs, axis=-1, keepdims=True)
        flat_e = k_idx.reshape(-1)
        onehot = jax.nn.one_hot(flat_e, E, dtype=jnp.int32)
        rank = jnp.take_along_axis(jnp.cumsum(onehot, axis=0) - 1, flat_e[:, None], axis=1)[:, 0]
        keep = rank < capacity
        slot = jnp.minimum(rank, capacity - 1)
        token_id = jnp.arange(P) // K
        dispatched = jnp.where(keep[:, None], xf[token_id], 0.0)
        buf = jnp.zeros((E, capacity, H), x.dtype).at[flat_e, slot].add(dispatched)
        h = jax.nn.silu(jnp.einsum('ech,ehf->ecf', buf, w1))
        out_buf = jnp.einsum('ecf,efh->ech', h, w2)
        pair_out = out_buf[flat_e, slot] * keep[:, None].astype(x.dtype)
        combined = jnp.sum(pair_out.reshape(N, K, H) * k_probs[..., None], axis=1)
        return combined.reshape(B, T, H) + x
    x = x + _L0_attn_ref(_layernorm(x, axis=-1), L0_attn_w1, L0_attn_w2, L0_attn_w3, L0_attn_conv_w, L0_attn_conv_b, L0_attn_A_w, L0_attn_A_b, L0_attn_B_w, L0_attn_B_b, L0_attn_C_w, L0_attn_C_b, L0_attn_D_w, L0_attn_D_b, L0_attn_dl_w, L0_attn_dl_b)
    x = x + _L0_xattn_ref(_layernorm(x, axis=-1), ctx_1024, ctx_1024, L0_xattn_WQ, L0_xattn_bQ, L0_xattn_WK, L0_xattn_bK, L0_xattn_WV, L0_xattn_bV, L0_xattn_WO, L0_xattn_bO)
    x = x + _L0_ffn_ref(_layernorm(x, axis=-1), L0_ffn_router_w, L0_ffn_w1, L0_ffn_w2)
    return x

_drawn_inputs = setup_inputs


def setup_inputs(seed=0):
    import zlib

    import numpy as np

    out = dict(_drawn_inputs(seed))
    spreads = {'L0_attn_A_b': (1.0, 0.2),
     'L0_attn_B_b': (0.0, 0.1),
     'L0_attn_C_b': (0.0, 0.347),
     'L0_attn_D_b': (0.0, 0.342),
     'L0_attn_dl_b': (-5.0, 0.2)}
    factors = {'L0_attn_w1': 7.329,
     'L0_attn_conv_w': 6.799,
     'L0_attn_A_w': 8.0,
     'L0_attn_D_w': 8.0,
     'L0_attn_dl_w': 8.0,
     'L0_xattn_bQ': 42.527,
     'L0_xattn_bK': 64.0,
     'L0_xattn_bV': 15.361,
     'L0_xattn_bO': 14.748,
     'L0_ffn_router_w': 6.575,
     'L0_ffn_w1': 6.319,
     'L0_ffn_w2': 6.099,
     'L0_attn_conv_b': 3.255,
     'L0_xattn_WQ': 3.07}
    for name, (base, spread) in spreads.items():
        noise = np.random.default_rng([zlib.crc32(name.encode()), seed]).standard_normal(out[name].shape)
        drawn = base * np.exp(spread * noise) if base else spread * noise
        out[name] = jnp.asarray(drawn.astype(out[name].dtype))
    for name, factor in factors.items():
        out[name] = (out[name] * factor).astype(out[name].dtype)
    return out
```

```python
from contextlib import ExitStack

import concourse.bass as bass
from concourse import mybir

F32 = mybir.dt.float32
F32R = mybir.dt.float32r
BF16 = mybir.dt.bfloat16
F16 = mybir.dt.float16
U32 = mybir.dt.uint32
ALU = mybir.AluOpType
ACT = mybir.ActivationFunctionType
AX = mybir.AxisListType

P = 128
B, L, D = 8, 256, 256
N = B * L
DC = D // P
NT = N // P
BLK = 512
TPB = BLK // P
NBLK = N // BLK
HID = 512
HC = HID // P
HEADS, HD = 16, 16
SCALE = 1.0 / HD ** 0.5
E, K, FF = 8, 2, 1024
FC = FF // P
CAP = int(1.25 * N * K / E) + 1
ST = 6
SP_ = -(-CAP // (ST * 4)) * 4
SLOTS = ST * SP_
HALF = SLOTS // 2
FAR = 1 << 20
EPS = 1e-5
NEG = -1e30
VW = HD + 1

MIX = {}
_at = 0
for _name, _kc, _out in (("w1", DC, D), ("w2", DC, D), ("w3", DC, D), ("D_w", DC, D),
                         ("dl_w", DC, HID), ("A_w", DC, HID), ("B_w", DC, HID), ("C_w", HC, D)):
    MIX[_name] = (_at, _kc, _out)
    _at += _kc * _out
MIXW = _at


class Sems:

    def __init__(self, ctx, nc, prefix):
        self.ctx, self.nc, self.prefix, self.made = ctx, nc, prefix, {}

    def __getitem__(self, name):
        if name not in self.made:
            self.made[name] = self.ctx.enter_context(self.nc.semaphore(f"{self.prefix}_{name}"))
        return self.made[name]


START_AT_ONE = {
    "m": ("C", "conv", "hl", "w1", "x_out", "zl"),
    "q": ("cT", "k_out", "q", "q_out", "v", "vf", "vr", "xT"),
    "a": ("exp", "kx", "o", "pl", "pv", "turned", "s0", "s1"),
    "w": ("lg", "lg_out", "ol", "x2", "x2_out", "x3_out", "xT", "xt", "y", "ya"),
    "f": ("h", "hh", "hl", "rows_used", "stored", "v", "w1l", "w2l", "xl", "y", "y_out"),
}


def memory(ctx, nc, prefix):
    def sb(name, shape, dt=F32):
        return ctx.enter_context(nc.sbuf_tensor(f"{prefix}_{name}", shape, dt))

    def pb(name, shape, dt=F32):
        return ctx.enter_context(nc.psum_tensor(f"{prefix}_{name}", shape, dt))

    return sb, pb


def split_product(pe, out, parts, first=True, last=True):
    n = 0
    for (lh, ll), (rh, rl) in parts:
        for a, b in ((lh, rh), (lh, rl), (ll, rh)):
            mm = pe.matmul(out, a, b, start=first and n == 0, stop=last and n == 3 * len(parts) - 1)
            n += 1
    return mm


def variance_and_mean(dve, S, st, mom, ve, i):
    dve.tensor_tensor(mom[:, 1, :], st[:, :, 1], st[:, :, 4], ALU.add).then_inc(S["mom"], 1)
    dve.tensor_tensor(mom[:, 2, :], st[:, :, 1], st[:, :, 4], ALU.subtract).then_inc(S["mom"], 1)
    dve.tensor_tensor(mom[:, 3, :], st[:, :, 2], st[:, :, 5], ALU.add).then_inc(S["mom"], 1)
    dve.wait_ge(S["mom"], 5 * i + 3)
    dve.tensor_scalar(mom[:, 0, :], mom[:, 1, :], 0.5, None, ALU.mult).then_inc(S["mean"], 1)
    dve.scalar_tensor_tensor(mom[:, 2, :], mom[:, 2, :], 0.25, mom[:, 2, :], ALU.mult, ALU.mult).then_inc(S["mom"], 1)
    dve.tensor_scalar(mom[:, 3, :], mom[:, 3, :], 1.0 / D, EPS, ALU.mult, ALU.add).then_inc(S["mom"], 1)
    dve.wait_ge(S["mom"], 5 * i + 5)
    dve.wait_ge(S["mean"], i + 1)
    dve.tensor_tensor(ve[:, :], mom[:, 2, :], mom[:, 3, :], ALU.add).then_inc(S["ve"], 1)


def constants(nc, ctx, sems):
    sb, _ = memory(ctx, nc, "c")
    S = sems["c"]
    c = {
        "ident": sb("ident", [P, P]), "identb": sb("identb", [P, P], BF16),
        "place": sb("place", [P, DC, D], F32R),
        "mask": sb("mask", [P, P], BF16), "head": sb("head", [P, P // HD]),
        "ones": sb("ones", [P, P]), "before": sb("before", [P, P]),
        "zero": sb("zeros", [SP_, ST, D]),
        "mhalf": sb("mhalf", [P, TPB]), "iota": sb("iota", [P, E]),
    }
    place32 = sb("place32", [P, DC, D])
    with nc.Block() as block:

        @block.sync
        def _(sp):
            for phase, names in START_AT_ONE.items():
                for name in names:
                    sp.sem_inc(sems[phase][name], 1)

        @block.gpsimd
        def _(pool):
            pool.memset(c["ident"][:, :], 0.0).then_inc(S["zero"], 1)
            pool.memset(c["identb"][:, :], 0.0).then_inc(S["zero"], 1)
            pool.memset(place32[:, :, :], 0.0).then_inc(S["zero"], 1)
            pool.memset(c["mask"][:, :], 0.0).then_inc(S["zero"], 1)
            pool.memset(c["head"][:, :], 1.0).then_inc(S["zero"], 1)
            pool.memset(c["ones"][:, :], 1.0).then_inc(S["zero"], 1)
            pool.memset(c["before"][:, :], 1.0).then_inc(S["zero"], 1)
            pool.memset(c["mhalf"][:, :], -0.5).then_inc(S["zero"], 1)
            pool.memset(c["zero"][:, :, :], 0.0).then_inc(S["zero"], 1)
            for e in range(E):
                pool.memset(c["iota"][:, e:e + 1], float(e)).then_inc(S["zero"], 1)
            pool.wait_ge(S["zero"], 9 + E)
            for m in (c["ident"], c["identb"]):
                pool.affine_select(out=m[:, :], in_=m[:, :], compare_op=ALU.not_equal, fill=1.0, base=0,
                                   pattern=[[-1, P]], channel_multiplier=1).then_inc(S["made"], 1)
            for k in range(DC):
                v = place32[:, k, k * P:(k + 1) * P]
                pool.affine_select(out=v, in_=v, compare_op=ALU.not_equal, fill=1.0, base=0,
                                   pattern=[[-1, P]], channel_multiplier=1).then_inc(S["made"], 1)
            pool.affine_select(out=c["mask"][:, :], in_=c["mask"][:, :], compare_op=ALU.is_ge, fill=NEG,
                               base=0, pattern=[[-1, P]], channel_multiplier=1).then_inc(S["made"], 1)
            pool.affine_select(out=c["before"][:, :], in_=c["before"][:, :], compare_op=ALU.is_ge,
                               fill=0.0, base=-1, pattern=[[1, P]], channel_multiplier=-1).then_inc(S["made"], 1)
            pool.affine_select(out=c["head"][:, :], in_=c["head"][:, :], compare_op=ALU.is_ge, fill=0.0,
                               base=0, pattern=[[-HD, P // HD]], channel_multiplier=1).then_inc(S["head"], 1)
            pool.wait_ge(S["head"], 1)
            pool.affine_select(out=c["head"][:, :], in_=c["head"][:, :], compare_op=ALU.is_ge, fill=0.0,
                               base=HD - 1, pattern=[[HD, P // HD]], channel_multiplier=-1).then_inc(S["made"], 1)

        @block.vector
        def _(dve):
            dve.wait_ge(S["made"], 4)
            dve.tensor_copy(c["place"][:, :, :], place32[:, :, :]).then_inc(S["made"], 1)
            dve.wait_ge(S["made"], 8)

    return c


def mixer(nc, sems, c, x_sb, x, w, vec):
    with ExitStack() as ctx:
        sb, pb = memory(ctx, nc, "m")
        S = sems["m"]
        wst = sb("wst", [P, MIXW])
        wh, wl = sb("wh", [P, MIXW], F32R), sb("wl", [P, MIXW], F32R)
        cw, cb = sb("cw", [P, DC, 3]), sb("cb", [P, DC])
        dlb, Ab, Bb = sb("dlb", [P, HC]), sb("Ab", [P, HC]), sb("Bb", [P, HC])
        Cb, Db, CDb = sb("Cb", [P, DC]), sb("Db", [P, DC]), sb("CDb", [P, DC])
        xin = sb("xin", [P, TPB, D])
        xn = sb("xn", [P, TPB, D])
        st, mom = sb("st", [P, TPB, 6]), sb("mom", [P, 4, TPB])
        ve, rstd = sb("ve", [P, TPB]), sb("rstd", [P, TPB])
        xh, xl = sb("xh", [P, DC, BLK], F32R), sb("xl", [P, DC, BLK], F32R)
        ypad = sb("ypad", [P, DC, 2, L + 2])
        cv, th = sb("cv", [P, DC, BLK]), sb("th", [P, DC, BLK])
        sh, sl = sb("sh", [P, DC, BLK], F32R), sb("sl", [P, DC, BLK], F32R)
        e, a, hs = sb("e", [P, HC, BLK]), sb("a", [P, HC, BLK]), sb("hs", [P, HC, BLK])
        hh, hl = sb("hh", [P, HC, BLK], F32R), sb("hl", [P, HC, BLK], F32R)
        ssm = sb("ssm", [P, DC, BLK])
        banks = [pb(f"bank{n}", [P, BLK]) for n in range(8)]

        def weights(name, k, m0, m):
            at, _, out = MIX[name]
            s = slice(at + k * out + m0, at + k * out + m0 + m)
            return wh[:, s], wl[:, s]

        with nc.Block() as block:

            @block.sync
            def _(sp):
                for name, (at, kc, out) in MIX.items():
                    sp.dma_start(wst[:, at:at + kc * out].rearrange("p (k o) -> p k o", k=kc),
                                 w[name].rearrange("(k p) o -> p k o", p=P)).then_inc(S["w_in"], 16)
                small = ((cw, vec["conv_w"].rearrange("(k p) t -> p k t", p=P)),
                         (cb, vec["conv_b"]),
                         (dlb, vec["dl_b"]),
                         (Ab, vec["A_b"]),
                         (Bb, vec["B_b"]),
                         (Cb, vec["C_b"]),
                         (Db, vec["D_b"]))
                for dst, src in small:
                    sp.dma_start(dst[:], src).then_inc(S["v_in"], 16)
                with sp.Fori(0, NBLK) as i:
                    sp.wait_ge(S["x_out"], 1 + TPB * i)
                    sp.dma_start(xin[:, :, :], x[bass.ds(i * BLK, BLK), :].rearrange("(t p) d -> p t d", p=P))\
                        .then_inc(S["x_in"], 16)

            @block.gpsimd
            def _(pool):
                pool.memset(ypad[:, :, :, :], 0.0).then_inc(S["pad"], 1)
                pool.wait_ge(S["w_in"], 16 * len(MIX))
                pool.wait_ge(S["wh"], 1)
                pool.tensor_tensor(wl[:, :], wst[:, :], wh[:, :].bitcast(F32), ALU.subtract).then_inc(S["wl"], 1)
                with pool.Fori(0, NBLK) as i:
                    pool.wait_ge(S["ve"], i + 1)
                    pool.tensor_tensor(rstd[:, :], ve[:, :], c["mhalf"][:, :], ALU.pow).then_inc(S["rstd"], 1)
                    for m in range(HC):
                        pool.wait_ge(S["hh"], HC * i + m + 1)
                        pool.wait_ge(S["C"], 1 + DC * i)
                        pool.tensor_tensor(hl[:, m, :], hs[:, m, :], hh[:, m, :].bitcast(F32), ALU.subtract)\
                            .then_inc(S["hl"], 1)

            @block.scalar
            def _(act):
                act.wait_ge(S["w_in"], 16 * len(MIX))
                act.activation(wh[:, :], wst[:, :], ACT.Copy).then_inc(S["wh"], 1)
                act.wait_ge(S["pad"], 1)
                act.wait_ge(S["v_in"], 16 * 7)
                with act.Fori(0, NBLK) as i:
                    for k in range(DC):
                        act.wait_ge(S["xT"], DC * i + k + 1)
                        act.wait_ge(S["w1"], 1 + DC * i)
                        act.activation(xh[:, k, :], banks[k][:, :], ACT.Copy).then_inc(S["xh"], 1)
                    for m in range(DC):
                        act.wait_ge(S["w1"], 1 + DC * i + m + 1)
                        act.wait_ge(S["conv"], 1 + DC * i)
                        act.activation(ypad[:, m, :, 1:L + 1],
                                       banks[2 + m][:, :].rearrange("p (b l) -> p b l", b=2),
                                       ACT.Copy).then_inc(S["y"], 1)
                    for m in range(DC):
                        act.wait_ge(S["conv"], 1 + DC * i + m + 1)
                        act.activation(th[:, m, :], cv[:, m, :], ACT.Tanh, scale=0.5).then_inc(S["th"], 1)
                    for m in range(DC):
                        act.wait_ge(S["silu"], DC * i + m + 1)
                        act.wait_ge(S["C"], 1 + DC * i)
                        act.activation(sh[:, m, :], cv[:, m, :], ACT.Copy, scale=0.5).then_inc(S["sh"], 1)
                    for m in range(HC):
                        act.wait_ge(S["dmin"], HC * i + m + 1)
                        act.activation(e[:, m, :], e[:, m, :], ACT.Exp).then_inc(S["dexp"], 1)
                    for m in range(HC):
                        act.wait_ge(S["dexp"], HC * i + m + 1)
                        act.activation(e[:, m, :], e[:, m, :], ACT.Ln, bias=1.0).then_inc(S["dln"], 1)
                    for m in range(HC):
                        act.wait_ge(S["dA"], HC * i + m + 1)
                        act.activation(e[:, m, :], e[:, m, :], ACT.Exp, scale=-1.0).then_inc(S["abar"], 1)
                    for m in range(HC):
                        act.wait_ge(S["h"], HC * i + m + 1)
                        act.wait_ge(S["C"], 1 + DC * i)
                        act.activation(hh[:, m, :], hs[:, m, :], ACT.Copy).then_inc(S["hh"], 1)
                    for m in range(DC):
                        act.wait_ge(S["C"], 1 + DC * i + m + 1)
                        act.wait_ge(S["bias"], 1)
                        act.activation(ssm[:, m, :], banks[4 + m][:, :], ACT.Identity, bias=CDb[:, m:m + 1])\
                            .then_inc(S["ssm"], 1)
                        act.wait_ge(S["ssm"], DC * i + m + 1)
                        act.activation(xh[:, m, :], ssm[:, m, :], ACT.Copy).then_inc(S["ssmh"], 1)
                    for m in range(DC):
                        act.wait_ge(S["w2"], DC * i + m + 1)
                        act.activation(th[:, m, :], banks[6 + m][:, :], ACT.Tanh, scale=0.5).then_inc(S["th2"], 1)
                    for m in range(DC):
                        act.wait_ge(S["z"], DC * i + m + 1)
                        act.activation(sh[:, m, :], cv[:, m, :], ACT.Copy, scale=0.5).then_inc(S["zh"], 1)

            @block.tensor
            def _(pe):
                pe.wait_ge(S["wl"], 1)
                with pe.Fori(0, NBLK) as i:
                    for k in range(DC):
                        pe.wait_ge(S["x_out"], 1 + TPB * i)
                        for t in range(TPB):
                            pe.wait_ge(S["xn"], TPB * i + t + 1)
                            mm = pe.transpose(banks[k][:, t * P:(t + 1) * P], xn[:, t, k * P:(k + 1) * P],
                                              c["ident"][:, :])
                        mm.then_inc(S["xT"], 1)
                    pe.wait_ge(S["xh"], DC * (i + 1))
                    pe.wait_ge(S["xl"], DC * (i + 1))
                    for m in range(DC):
                        split_product(pe, banks[2 + m][:, :],
                                      [(weights("w1", k, m * P, P), (xh[:, k, :], xl[:, k, :])) for k in range(DC)])\
                            .then_inc(S["w1"], 1)
                    xs = [(sh[:, k, :], sl[:, k, :]) for k in range(DC)]
                    pe.wait_ge(S["sh"], DC * (i + 1))
                    pe.wait_ge(S["sl"], DC * (i + 1))
                    for m in range(HC):
                        split_product(pe, banks[m][:, :],
                                      [(weights("dl_w", k, m * P, P), xs[k]) for k in range(DC)]).then_inc(S["dl"], 1)
                    for m in range(HC):
                        split_product(pe, banks[4 + m][:, :],
                                      [(weights("A_w", k, m * P, P), xs[k]) for k in range(DC)]).then_inc(S["A"], 1)
                    for m in range(HC):
                        pe.wait_ge(S["delta"], HC * i + m + 1)
                        split_product(pe, banks[m][:, :],
                                      [(weights("B_w", k, m * P, P), xs[k]) for k in range(DC)]).then_inc(S["Bx"], 1)
                    pe.wait_ge(S["hh"], HC * (i + 1))
                    pe.wait_ge(S["hl"], 1 + HC * (i + 1))
                    pe.wait_ge(S["dA"], HC * (i + 1))
                    for m in range(DC):
                        split_product(pe, banks[4 + m][:, :],
                                      [(weights("D_w", k, m * P, P), xs[k]) for k in range(DC)]
                                      + [(weights("C_w", k, m * P, P), (hh[:, k, :], hl[:, k, :])) for k in range(HC)])\
                            .then_inc(S["C"], 1)
                    pe.wait_ge(S["ssmh"], DC * (i + 1))
                    pe.wait_ge(S["ssml"], DC * (i + 1))
                    for m in range(DC):
                        split_product(pe, banks[6 + m][:, :],
                                      [(weights("w2", k, m * P, P), (xh[:, k, :], xl[:, k, :])) for k in range(DC)])\
                            .then_inc(S["w2"], 1)
                    pe.wait_ge(S["zh"], DC * (i + 1))
                    pe.wait_ge(S["zl"], 1 + DC * (i + 1))
                    for t in range(TPB):
                        out = banks[t][:, 0:D]
                        tok = slice(t * P, (t + 1) * P)
                        for k in range(DC):
                            pe.matmul(out, xh[:, k, tok], c["place"][:, k, :], start=k == 0, stop=False)
                            pe.matmul(out, xl[:, k, tok], c["place"][:, k, :], start=False, stop=False)
                        split_product(pe, out, [((sh[:, k, tok], sl[:, k, tok]), weights("w3", k, 0, D))
                                                for k in range(DC)], first=False).then_inc(S["w3"], 1)

            @block.vector
            def _(dve):
                dve.wait_ge(S["v_in"], 16 * 7)
                dve.tensor_tensor(CDb[:, :], Cb[:, :], Db[:, :], ALU.add).then_inc(S["bias"], 1)
                dve.wait_ge(S["pad"], 1)
                with dve.Fori(0, NBLK) as i:
                    dve.wait_ge(S["x_in"], 16 * (i + 1))
                    for t in range(TPB):
                        dve.bn_stats(st[:, t, :], xin[:, t, :]).then_inc(S["st"], 1)
                    dve.wait_ge(S["st"], TPB * (i + 1))
                    variance_and_mean(dve, S, st, mom, ve, i)
                    dve.wait_ge(S["rstd"], i + 1)
                    for t in range(TPB):
                        dve.tensor_scalar(xn[:, t, :], xin[:, t, :], mom[:, 0, t:t + 1], rstd[:, t:t + 1],
                                          ALU.subtract, ALU.mult).then_inc(S["xn"], 1)
                    for k in range(DC):
                        dve.wait_ge(S["xh"], DC * i + k + 1)
                        dve.tensor_tensor(xl[:, k, :], banks[k][:, :], xh[:, k, :].bitcast(F32), ALU.subtract)\
                            .then_inc(S["xl"], 1)
                    for m in range(DC):
                        dve.wait_ge(S["y"], DC * i + m + 1)
                        dve.wait_ge(S["zl"], 1 + DC * i)
                        acc = cv[:, m, :].rearrange("p (b l) -> p b l", b=2)
                        dve.tensor_scalar(acc, ypad[:, m, :, 1:L + 1], cw[:, m, 1:2], cb[:, m:m + 1],
                                          ALU.mult, ALU.add).then_inc(S["tap"], 1)
                        dve.wait_ge(S["tap"], 2 * (DC * i + m) + 1)
                        dve.scalar_tensor_tensor(acc, ypad[:, m, :, 0:L], cw[:, m, 0:1], acc, ALU.mult, ALU.add)\
                            .then_inc(S["tap"], 1)
                        dve.wait_ge(S["tap"], 2 * (DC * i + m) + 2)
                        dve.scalar_tensor_tensor(acc, ypad[:, m, :, 2:L + 2], cw[:, m, 2:3], acc, ALU.mult, ALU.add)\
                            .then_inc(S["conv"], 1)
                    for m in range(DC):
                        dve.wait_ge(S["th"], DC * i + m + 1)
                        dve.scalar_tensor_tensor(cv[:, m, :], th[:, m, :], 1.0, cv[:, m, :], ALU.add, ALU.mult)\
                            .then_inc(S["silu"], 1)
                    for m in range(DC):
                        dve.wait_ge(S["sh"], DC * i + m + 1)
                        dve.scalar_tensor_tensor(sl[:, m, :], cv[:, m, :], 0.5, sh[:, m, :].bitcast(F32),
                                                 ALU.mult, ALU.subtract).then_inc(S["sl"], 1)
                    for m in range(HC):
                        dve.wait_ge(S["dl"], HC * i + m + 1)
                        dve.tensor_scalar(e[:, m, :], banks[m][:, :], dlb[:, m:m + 1], 40.0, ALU.add, ALU.min)\
                            .then_inc(S["dmin"], 1)
                    for m in range(HC):
                        dve.wait_ge(S["dln"], HC * i + m + 1)
                        dve.scalar_tensor_tensor(e[:, m, :], banks[m][:, :], dlb[:, m:m + 1], e[:, m, :],
                                                 ALU.add, ALU.max).then_inc(S["delta"], 1)
                    for m in range(HC):
                        dve.wait_ge(S["A"], HC * i + m + 1)
                        dve.wait_ge(S["delta"], HC * i + m + 1)
                        dve.scalar_tensor_tensor(e[:, m, :], banks[4 + m][:, :], Ab[:, m:m + 1], e[:, m, :],
                                                 ALU.add, ALU.mult).then_inc(S["dA"], 1)
                    for m in range(HC):
                        dve.wait_ge(S["abar"], HC * i + m + 1)
                        for b in range(2):
                            s = slice(b * L, (b + 1) * L)
                            dve.tensor_tensor_scan(a[:, m, s], e[:, m, s], e[:, m, s], 1.0, ALU.mult, ALU.bypass)\
                                .then_inc(S["acum"], 1)
                        dve.wait_ge(S["acum"], 2 * (HC * i + m + 1))
                        dve.wait_ge(S["Bx"], HC * i + m + 1)
                        dve.scalar_tensor_tensor(a[:, m, :], banks[m][:, :], Bb[:, m:m + 1], a[:, m, :],
                                                 ALU.add, ALU.mult).then_inc(S["Ba"], 1)
                        dve.wait_ge(S["Ba"], HC * i + m + 1)
                        dve.wait_ge(S["hl"], 1 + HC * i)
                        for b in range(2):
                            s = slice(b * L, (b + 1) * L)
                            ins = dve.tensor_tensor_scan(hs[:, m, s], a[:, m, s], a[:, m, s], 0.0, ALU.add, ALU.bypass)
                        ins.then_inc(S["h"], 1)
                    for m in range(DC):
                        dve.wait_ge(S["ssmh"], DC * i + m + 1)
                        dve.tensor_tensor(xl[:, m, :], ssm[:, m, :], xh[:, m, :].bitcast(F32), ALU.subtract)\
                            .then_inc(S["ssml"], 1)
                    for m in range(DC):
                        dve.wait_ge(S["th2"], DC * i + m + 1)
                        dve.scalar_tensor_tensor(cv[:, m, :], th[:, m, :], 1.0, banks[6 + m][:, :], ALU.add, ALU.mult)\
                            .then_inc(S["g"], 1)
                        dve.wait_ge(S["g"], DC * i + m + 1)
                        dve.tensor_tensor(cv[:, m, :], cv[:, m, :], ssm[:, m, :], ALU.mult).then_inc(S["z"], 1)
                    for m in range(DC):
                        dve.wait_ge(S["zh"], DC * i + m + 1)
                        dve.scalar_tensor_tensor(sl[:, m, :], cv[:, m, :], 0.5, sh[:, m, :].bitcast(F32),
                                                 ALU.mult, ALU.subtract).then_inc(S["zl"], 1)
                    for t in range(TPB):
                        dve.wait_ge(S["w3"], TPB * i + t + 1)
                        dve.tensor_tensor(x_sb[:, bass.ds((TPB * i + t) * D, D)],
                                          banks[t][:, 0:D],
                                          xin[:, t, :], ALU.add).then_inc(S["x_out"], 1)
                dve.wait_ge(S["x_out"], 1 + NT)


def load_split(sp_eng, S, wst, parts):
    at = 0
    for src in parts:
        kc, out = src.shape[0] // P, src.shape[1]
        sp_eng.dma_start(wst[:, at:at + kc * out].rearrange("p (k o) -> p k o", k=kc),
                         src.rearrange("(k p) o -> p k o", p=P)).then_inc(S["w_in"], 16)
        at += kc * out


def projections(nc, sems, c, x_sb, ctx_in, w, vec, qt, kt, vs, woh, wol, bo):
    with ExitStack() as ctx:
        sb, pb = memory(ctx, nc, "q")
        S = sems["q"]
        WW = DC * D
        wst = sb("wst", [P, 4 * WW])
        wh, wl = sb("wh", [P, 3 * WW], F32R), sb("wl", [P, 3 * WW], F32R)
        bq, bk = sb("bq", [P, DC]), sb("bk", [P, DC])
        brow = sb("brow", [1, 2 * D])
        bv = sb("bv", [P, D])
        cin = sb("cin", [P, TPB, D])
        xn = sb("xn", [P, TPB, D])
        st, mom = sb("st", [P, TPB, 6]), sb("mom", [P, 4, TPB])
        ve, rstd = sb("ve", [P, TPB]), sb("rstd", [P, TPB])
        xh, xl = sb("xh", [P, DC, BLK], F32R), sb("xl", [P, DC, BLK], F32R)
        ch, cl = sb("ch", [P, DC, BLK], F32R), sb("cl", [P, DC, BLK], F32R)
        vf, vr = sb("vf", [P, TPB, D]), sb("vr", [P, TPB, D])
        banks = [pb(f"bank{n}", [P, BLK]) for n in range(8)]

        def weights(n, k, m0, m):
            s = slice(n * WW + k * D + m0, n * WW + k * D + m0 + m)
            return wh[:, s], wl[:, s]

        def v_part(tile, part):
            return vs[:, bass.ds(tile * (HEADS * 3 * VW), HEADS * 3 * VW)]\
                .rearrange("p (h a v) -> p h a v", h=HEADS, a=3)[:, :, part, 0:HD]

        with nc.Block() as block:

            @block.sync
            def _(sp):
                load_split(sp, S, wst, [w["WQ"], w["WK"], w["WV"], w["WO"]])
                sp.dma_start(bq[:, :], vec["bQ"]).then_inc(S["v_in"], 16)
                sp.dma_start(bk[:, :], vec["bK"]).then_inc(S["v_in"], 16)
                sp.dma_start(brow[:, 0:D], vec["bV"]).then_inc(S["v_in"], 16)
                sp.dma_start(brow[:, D:2 * D], vec["bO"]).then_inc(S["v_in"], 16)
                with sp.Fori(0, NBLK) as i:
                    sp.wait_ge(S["cT"], 1 + DC * i)
                    sp.dma_start(cin[:, :, :], ctx_in[bass.ds(i * BLK, BLK), :]
                                 .rearrange("(t p) d -> p t d", p=P)).then_inc(S["c_in"], 16)

            @block.gpsimd
            def _(pool):
                pool.memset(vs[:, :], 0.0).then_inc(S["vzero"], 1)
                pool.wait_ge(S["vzero"], 1)
                ones = vs[:, :].rearrange("p (n a v) -> p n a v", a=3, v=VW)[:, :, 0, HD:VW]
                pool.memset(ones, 1.0).then_inc(S["vzero"], 1)
                pool.wait_ge(S["w_in"], 16 * 4)
                pool.wait_ge(S["wh"], 2)
                pool.tensor_tensor(wl[:, :], wst[:, 0:3 * WW], wh[:, :].bitcast(F32), ALU.subtract)\
                    .then_inc(S["wl"], 1)
                pool.tensor_tensor(wol[:, :], wst[:, 3 * WW:4 * WW], woh[:, :].bitcast(F32), ALU.subtract)\
                    .then_inc(S["wl"], 1)
                with pool.Fori(0, NBLK) as i:
                    pool.wait_ge(S["ve"], i + 1)
                    pool.tensor_tensor(rstd[:, :], ve[:, :], c["mhalf"][:, :], ALU.pow).then_inc(S["rstd"], 1)
                    for t in range(TPB):
                        tile = TPB * i + t
                        pool.wait_ge(S["v1"], tile + 1)
                        pool.tensor_tensor(vr[:, t, :].rearrange("p (h v) -> p h v", h=HEADS),
                                           vf[:, t, :].rearrange("p (h v) -> p h v", h=HEADS),
                                           v_part(tile, 0), ALU.subtract).then_inc(S["vr"], 1)
                        pool.wait_ge(S["v2"], tile + 1)
                        pool.tensor_tensor(v_part(tile, 2), vr[:, t, :].rearrange("p (h v) -> p h v", h=HEADS),
                                           v_part(tile, 1), ALU.subtract).then_inc(S["v3"], 1)
                pool.wait_ge(S["v3"], NT)

            @block.scalar
            def _(act):
                act.wait_ge(S["w_in"], 16 * 4)
                act.activation(wh[:, :], wst[:, 0:3 * WW], ACT.Copy).then_inc(S["wh"], 1)
                act.activation(woh[:, :], wst[:, 3 * WW:4 * WW], ACT.Copy).then_inc(S["wh"], 1)
                act.wait_ge(S["v_in"], 16 * 4)
                act.wait_ge(S["vzero"], 2)
                with act.Fori(0, NBLK) as i:
                    for k in range(DC):
                        act.wait_ge(S["xT"], 1 + DC * i + k + 1)
                        act.wait_ge(S["q"], 1 + DC * i)
                        act.activation(xh[:, k, :], banks[k][:, :], ACT.Copy).then_inc(S["xh"], 1)
                    for k in range(DC):
                        act.wait_ge(S["cT"], 1 + DC * i + k + 1)
                        act.wait_ge(S["v"], 1 + TPB * i)
                        act.activation(ch[:, k, :], banks[2 + k][:, :], ACT.Copy).then_inc(S["ch"], 1)
                    for m in range(DC):
                        act.wait_ge(S["q"], 1 + DC * i + m + 1)
                        act.activation(qt[:, bass.ds(m * N + i * BLK, BLK)], banks[4 + m][:, :],
                                       ACT.Identity, bias=bq[:, m:m + 1]).then_inc(S["q_out"], 1)
                    for m in range(DC):
                        act.wait_ge(S["k"], DC * i + m + 1)
                        act.activation(kt[:, bass.ds(m * N + i * BLK, BLK)], banks[6 + m][:, :],
                                       ACT.Identity, bias=bk[:, m:m + 1]).then_inc(S["k_out"], 1)
                    for t in range(TPB):
                        tile = TPB * i + t
                        act.wait_ge(S["vf"], 1 + tile + 1)
                        act.activation(v_part(tile, 0), vf[:, t, :].rearrange("p (h v) -> p h v", h=HEADS),
                                       ACT.Copy).then_inc(S["v1"], 1)
                    for t in range(TPB):
                        tile = TPB * i + t
                        act.wait_ge(S["vr"], 1 + tile + 1)
                        act.activation(v_part(tile, 1), vr[:, t, :].rearrange("p (h v) -> p h v", h=HEADS),
                                       ACT.Copy).then_inc(S["v2"], 1)

            @block.tensor
            def _(pe):
                pe.wait_ge(S["v_in"], 16 * 4)
                pe.matmul(banks[0][:, 0:D], c["ones"][0:1, :], brow[:, 0:D], start=True, stop=True)\
                    .then_inc(S["brows"], 1)
                pe.matmul(banks[1][:, 0:D], c["ones"][0:1, :], brow[:, D:2 * D], start=True, stop=True)\
                    .then_inc(S["brows"], 1)
                pe.wait_ge(S["wl"], 2)
                pe.wait_ge(S["bvo"], 2)
                with pe.Fori(0, NBLK) as i:
                    pe.wait_ge(S["vf"], 1 + TPB * i)
                    for k in range(DC):
                        for t in range(TPB):
                            pe.wait_ge(S["xn"], TPB * i + t + 1)
                            mm = pe.transpose(banks[k][:, t * P:(t + 1) * P], xn[:, t, k * P:(k + 1) * P],
                                              c["ident"][:, :])
                        mm.then_inc(S["xT"], 1)
                    pe.wait_ge(S["c_in"], 16 * (i + 1))
                    for k in range(DC):
                        for t in range(TPB):
                            mm = pe.transpose(banks[2 + k][:, t * P:(t + 1) * P], cin[:, t, k * P:(k + 1) * P],
                                              c["ident"][:, :])
                        mm.then_inc(S["cT"], 1)
                    pe.wait_ge(S["xh"], DC * (i + 1))
                    pe.wait_ge(S["xl"], DC * (i + 1))
                    pe.wait_ge(S["q_out"], 1 + DC * i)
                    for m in range(DC):
                        split_product(pe, banks[4 + m][:, :],
                                      [(weights(0, k, m * P, P), (xh[:, k, :], xl[:, k, :])) for k in range(DC)])\
                            .then_inc(S["q"], 1)
                    pe.wait_ge(S["ch"], DC * (i + 1))
                    pe.wait_ge(S["cl"], DC * (i + 1))
                    pe.wait_ge(S["k_out"], 1 + DC * i)
                    for m in range(DC):
                        split_product(pe, banks[6 + m][:, :],
                                      [(weights(1, k, m * P, P), (ch[:, k, :], cl[:, k, :])) for k in range(DC)])\
                            .then_inc(S["k"], 1)
                    for t in range(TPB):
                        tok = slice(t * P, (t + 1) * P)
                        split_product(pe, banks[t][:, 0:D],
                                      [((ch[:, k, tok], cl[:, k, tok]), weights(2, k, 0, D)) for k in range(DC)])\
                            .then_inc(S["v"], 1)

            @block.vector
            def _(dve):
                dve.wait_ge(S["brows"], 2)
                dve.tensor_copy(bv[:, :], banks[0][:, 0:D]).then_inc(S["bvo"], 1)
                dve.tensor_copy(bo[:, :], banks[1][:, 0:D]).then_inc(S["bvo"], 1)
                dve.wait_ge(S["bvo"], 2)
                with dve.Fori(0, NBLK) as i:
                    for t in range(TPB):
                        dve.bn_stats(st[:, t, :], x_sb[:, bass.ds((TPB * i + t) * D, D)]).then_inc(S["st"], 1)
                    dve.wait_ge(S["st"], TPB * (i + 1))
                    variance_and_mean(dve, S, st, mom, ve, i)
                    dve.wait_ge(S["rstd"], i + 1)
                    dve.wait_ge(S["xT"], 1 + DC * i)
                    for t in range(TPB):
                        dve.tensor_scalar(xn[:, t, :], x_sb[:, bass.ds((TPB * i + t) * D, D)], mom[:, 0, t:t + 1],
                                          rstd[:, t:t + 1], ALU.subtract, ALU.mult).then_inc(S["xn"], 1)
                    for k in range(DC):
                        dve.wait_ge(S["xh"], DC * i + k + 1)
                        dve.tensor_tensor(xl[:, k, :], banks[k][:, :], xh[:, k, :].bitcast(F32), ALU.subtract)\
                            .then_inc(S["xl"], 1)
                    for k in range(DC):
                        dve.wait_ge(S["ch"], DC * i + k + 1)
                        dve.tensor_tensor(cl[:, k, :], banks[2 + k][:, :], ch[:, k, :].bitcast(F32), ALU.subtract)\
                            .then_inc(S["cl"], 1)
                    for t in range(TPB):
                        dve.wait_ge(S["v"], 1 + TPB * i + t + 1)
                        dve.wait_ge(S["vr"], 1 + TPB * i)
                        dve.tensor_tensor(vf[:, t, :], banks[t][:, 0:D], bv[:, :], ALU.add).then_inc(S["vf"], 1)


def attention(nc, sems, c, qt, kt, vs, o_sb):
    UPC = 6
    U = DC * UPC
    HPC = HEADS // DC

    def unit(u):
        k, r = divmod(u, UPC)
        return (k, 0, 4 * r, 4) if r < 2 else (k, 1, 2 * (r - 2), 2)

    last_of = {1: 0, 5: 1, 7: 2, 11: 3}

    with ExitStack() as ctx:
        sb, pb = memory(ctx, nc, "a")
        S = sems["a"]
        mask4 = sb("mask4", [P, 4, P], BF16)
        qb, kb = sb("qb", [P, DC, L]), sb("kb", [P, DC, L])
        kx = sb("kx", [P, DC, HPC, L])
        mx, nm = sb("mx", [P, U, 4]), sb("nm", [P, U, 4])
        pr = sb("pr", [P, 2, 4 * P])
        ph, pl = sb("ph", [P, 2, 4 * P], F16), sb("pl", [P, 2, 4 * P], F16)
        os, rc = sb("os", [P, 2, HPC, VW]), sb("rc", [P, 2, HPC])
        sbank = [pb(f"scores{n}", [P, 4 * P]) for n in range(3)]
        tbank = [pb(f"turned{n}", [P, 4 * P]) for n in range(2)]
        obank = [pb(f"out{n}", [P, 4 * P]) for n in range(2)]

        with nc.Block() as block:

            @block.gpsimd
            def _(pool):
                for n in range(4):
                    pool.tensor_copy(mask4[:, n, :], c["mask"][:, :]).then_inc(S["mask"], 1)
                with pool.Fori(0, B) as b:
                    for k in range(DC):
                        pool.wait_ge(S["kb"], DC * b + k + 1)
                        pool.wait_ge(S[f"s{k}"], 1 + UPC * b)
                        pool.tensor_tensor(kx[:, k, 0, :], kb[:, k, :], c["head"][:, 0:1].to_broadcast([P, L]), ALU.mult)\
                            .then_inc(S["kx0"], 1)
                        for h in range(1, HPC):
                            ins = pool.tensor_scalar(kx[:, k, h, :], kb[:, k, :], c["head"][:, h:h + 1], None, ALU.mult)
                        ins.then_inc(S["kx"], 1)

            @block.scalar
            def _(act):
                with act.Fori(0, B) as b:
                    for u in range(U + 1):
                        if u < U:
                            k, q, h0, nh = unit(u)
                            n = 4 * P // nh
                            act.wait_ge(S["nm"], U * b + u + 1)
                            act.wait_ge(S["turned"], 1 + U * b + u - 1 if u else U * b)
                            for j in range(nh):
                                ins = act.activation(pr[:, u % 2, j * n:(j + 1) * n], sbank[u % 3][:, j * n:(j + 1) * n],
                                                     ACT.Exp, bias=nm[:, u, j:j + 1], scale=SCALE)
                            ins.then_inc(S["exp"], 1)
                        if u >= 1:
                            v = u - 1
                            act.wait_ge(S["turned"], 1 + U * b + v + 1)
                            act.wait_ge(S["pv"], 1 + U * b + max(v - 1, 0))
                            act.activation(ph[:, v % 2, :], tbank[v % 2][:, :], ACT.Copy).then_inc(S["ph"], 1)

            @block.tensor
            def _(pe):
                def scores(b, u):
                    k, q, h0, nh = unit(u)
                    if u % UPC == 0:
                        pe.wait_ge(S["kx"], 1 + DC * b + k + 1)
                    pe.wait_ge(S["exp"], 1 + U * b + max(u - 2, 0))
                    keys = 4 * P // nh
                    out = sbank[u % 3][:, :].rearrange("p (h k) -> p h k", h=nh)
                    pe.matmul(out, qb[:, k, q * P:(q + 1) * P], kx[:, k, h0:h0 + nh, 0:keys], start=True, stop=False)
                    mm = pe.matmul(out[:, :, keys - P:keys], c["identb"][:, :], mask4[:, 0:nh, :], start=False, stop=True)
                    mm.then_inc(S[f"s{k}"], 1)

                def turn(b, u):
                    pe.wait_ge(S["exp"], 1 + U * b + u + 1)
                    pe.wait_ge(S["pl"], 1 + U * b + max(u - 1, 0))
                    for j in range(4):
                        mm = pe.transpose(tbank[u % 2][:, j * P:(j + 1) * P], pr[:, u % 2, j * P:(j + 1) * P],
                                          c["ident"][:, :])
                    mm.then_inc(S["turned"], 1)

                def weigh(b, u):
                    k, q, h0, nh = unit(u)
                    pe.wait_ge(S["ph"], U * b + u + 1)
                    pe.wait_ge(S["pl"], 1 + U * b + u + 1)
                    g = 2 * k + q
                    if h0 == 0:
                        pe.wait_ge(S["o"], 1 + DC * 2 * b + max(g - 1, 0))
                    for j in range(nh):
                        out = obank[q][:, (h0 + j) * 3 * VW:(h0 + j + 1) * 3 * VW]
                        for t in range(q + 1):
                            v = vs[:, bass.ds(b * (2 * HEADS * 3 * VW) + (t * HEADS + k * HPC + h0 + j) * 3 * VW, 3 * VW)]
                            s = slice((j * (q + 1) + t) * P, (j * (q + 1) + t + 1) * P)
                            pe.matmul(out, ph[:, u % 2, s], v, start=t == 0, stop=False)
                            mm = pe.matmul(out, pl[:, u % 2, s], v, start=False, stop=t == q)
                    mm.then_inc(S["pv"], 1)

                pe.wait_ge(S["mask"], 4)
                with pe.Fori(0, B) as b:
                    scores(b, 0)
                    scores(b, 1)
                    for u in range(U + 1):
                        if u + 2 < U:
                            scores(b, u + 2)
                        if u < U:
                            turn(b, u)
                        if u >= 1:
                            weigh(b, u - 1)

            @block.vector
            def _(dve):
                with dve.Fori(0, B) as b:
                    for k in range(DC):
                        dve.wait_ge(S[f"s{k}"], 1 + UPC * b)
                        dve.tensor_copy(qb[:, k, :], qt[:, bass.ds(k * N + b * L, L)]).then_inc(S["qb"], 1)
                        dve.wait_ge(S["kx"], 1 + DC * b)
                        dve.tensor_copy(kb[:, k, :], kt[:, bass.ds(k * N + b * L, L)]).then_inc(S["kb"], 1)
                    for u in range(U + 2):
                        if u < U:
                            k, q, h0, nh = unit(u)
                            dve.wait_ge(S[f"s{k}"], 1 + UPC * b + u % UPC + 1)
                            dve.tensor_reduce(mx[:, u, 0:nh], sbank[u % 3][:, :].rearrange("p (h k) -> p h k", h=nh),
                                              AX.X, ALU.max).then_inc(S["mx"], 1)
                            dve.wait_ge(S["mx"], U * b + u + 1)
                            dve.wait_ge(S["exp"], 1 + U * b)
                            dve.tensor_scalar(nm[:, u, 0:nh], mx[:, u, 0:nh], -SCALE, None, ALU.mult).then_inc(S["nm"], 1)
                        if 1 <= u <= U:
                            v = u - 1
                            dve.wait_ge(S["ph"], U * b + v + 1)
                            dve.tensor_tensor(pl[:, v % 2, :], tbank[v % 2][:, :], ph[:, v % 2, :], ALU.subtract)\
                                .then_inc(S["pl"], 1)
                        if u >= 2 and u - 2 in last_of:
                            g = last_of[u - 2]
                            k, q = divmod(g, 2)
                            dve.wait_ge(S["pv"], 1 + U * b + u - 1)
                            dve.tensor_reduce(os[:, q, :, :], obank[q][:, 0:HPC * 3 * VW]
                                              .rearrange("p (h a v) -> p h v a", a=3, v=VW), AX.X, ALU.add)\
                                .then_inc(S["o"], 1)
                            dve.wait_ge(S["o"], 1 + 4 * b + g + 1)
                            dve.reciprocal(rc[:, q, :], os[:, q, :, HD]).then_inc(S["rc"], 1)
                            dve.wait_ge(S["rc"], 4 * b + g + 1)
                            dve.tensor_tensor(o_sb[:, bass.ds(b * (2 * D) + q * D + k * P, P)]
                                              .rearrange("p (h v) -> p h v", h=HPC),
                                              os[:, q, :, 0:HD], rc[:, q, :].unsqueeze(2).to_broadcast([P, HPC, HD]),
                                              ALU.mult).then_inc(S["on"], 1)
                dve.wait_ge(S["on"], 4 * B)


def output_and_router(nc, sems, c, x_sb, o_sb, x3, lg, woh, wol, bo, router_w):
    with ExitStack() as ctx:
        sb, pb = memory(ctx, nc, "w")
        S = sems["w"]
        rw = sb("rw", [P, DC, E])
        oh, ol = sb("oh", [P, DC, BLK], F32R), sb("ol", [P, DC, BLK], F32R)
        t1, t2 = sb("t1", [P, TPB, D]), sb("t2", [P, TPB, D])
        st, mom = sb("st", [P, TPB, 6]), sb("mom", [P, 4, TPB])
        ve, rstd = sb("ve", [P, TPB]), sb("rstd", [P, TPB])
        xt = sb("xt", [P, DC, BLK])
        ob, xb = [pb(f"ob{n}", [P, BLK]) for n in range(2)], [pb(f"xb{n}", [P, BLK]) for n in range(2)]
        yb = [pb(f"yb{n}", [P, BLK]) for n in range(3)]
        lb = pb("lb", [P, BLK])

        def tile(m, i, t):
            return m[:, bass.ds((TPB * i + t) * D, D)]

        with nc.Block() as block:

            @block.sync
            def _(sp):
                sp.dma_start(rw[:, :, :], router_w.rearrange("(k p) e -> p k e", p=P)).then_inc(S["rw"], 16)

            @block.gpsimd
            def _(pool):
                with pool.Fori(0, NBLK) as i:
                    pool.wait_ge(S["ve"], i + 1)
                    pool.tensor_tensor(rstd[:, :], ve[:, :], c["mhalf"][:, :], ALU.pow).then_inc(S["rstd"], 1)

            @block.scalar
            def _(act):
                with act.Fori(0, NBLK) as i:
                    for k in range(DC):
                        act.wait_ge(S["oT"], DC * i + k + 1)
                        act.wait_ge(S["y"], 1 + TPB * i)
                        act.activation(oh[:, k, :], ob[k][:, :], ACT.Copy).then_inc(S["oh"], 1)
                    for k in range(DC):
                        act.wait_ge(S["xT"], 1 + DC * i + k + 1)
                        act.wait_ge(S["lg"], 1 + i)
                        act.activation(xt[:, k, :], xb[k][:, :], ACT.Copy).then_inc(S["xt"], 1)
                    for t in range(TPB):
                        act.activation(tile(x_sb, i, t), t2[:, t, :], ACT.Copy).then_inc(S["x2_out"], 1)
                        act.activation(tile(x3, i, t), t1[:, t, :], ACT.Copy).then_inc(S["x3_out"], 1)
                act.wait_ge(S["x2_out"], 1 + NT)
                act.wait_ge(S["x3_out"], 1 + NT)

            @block.tensor
            def _(pe):
                pe.wait_ge(S["rw"], 16)
                with pe.Fori(0, NBLK) as i:
                    pe.wait_ge(S["ol"], 1 + DC * i)
                    for k in range(DC):
                        for t in range(TPB):
                            pe.wait_ge(S["o_tile"], TPB * i + t + 1)
                            mm = pe.transpose(ob[k][:, t * P:(t + 1) * P], t1[:, t, k * P:(k + 1) * P], c["ident"][:, :])
                        mm.then_inc(S["oT"], 1)
                    pe.wait_ge(S["oh"], DC * (i + 1))
                    pe.wait_ge(S["ol"], 1 + DC * (i + 1))
                    for t in range(TPB):
                        pe.wait_ge(S["ya"], 1 + TPB * i + max(t - 2, 0))
                        tok = slice(t * P, (t + 1) * P)
                        split_product(pe, yb[t % 3][:, 0:D],
                                      [((oh[:, k, tok], ol[:, k, tok]),
                                        (woh[:, k * D:(k + 1) * D], wol[:, k * D:(k + 1) * D])) for k in range(DC)])\
                            .then_inc(S["y"], 1)
                    pe.wait_ge(S["x3"], TPB * (i + 1))
                    pe.wait_ge(S["xt"], 1 + DC * i)
                    for k in range(DC):
                        for t in range(TPB):
                            mm = pe.transpose(xb[k][:, t * P:(t + 1) * P], t1[:, t, k * P:(k + 1) * P], c["ident"][:, :])
                        mm.then_inc(S["xT"], 1)
                    pe.wait_ge(S["xt"], 1 + DC * (i + 1))
                    pe.wait_ge(S["lg_out"], 1 + i)
                    for t in range(TPB):
                        for k in range(DC):
                            mm = pe.matmul(lb[:, t * E:(t + 1) * E], xt[:, k, t * P:(t + 1) * P], rw[:, k, :],
                                           start=k == 0, stop=k == DC - 1)
                    mm.then_inc(S["lg"], 1)

            @block.vector
            def _(dve):
                with dve.Fori(0, NBLK) as i:
                    for t in range(TPB):
                        dve.wait_ge(S["xT"], 1 + DC * i)
                        dve.wait_ge(S["x3_out"], 1 + TPB * i)
                        dve.tensor_copy(t1[:, t, :], tile(o_sb, i, t)).then_inc(S["o_tile"], 1)
                    for k in range(DC):
                        dve.wait_ge(S["oh"], DC * i + k + 1)
                        dve.tensor_tensor(ol[:, k, :], ob[k][:, :], oh[:, k, :].bitcast(F32), ALU.subtract)\
                            .then_inc(S["ol"], 1)
                    for t in range(TPB):
                        n = TPB * i + t + 1
                        dve.wait_ge(S["y"], 1 + n)
                        dve.tensor_tensor(t1[:, t, :], yb[t % 3][:, 0:D], bo[:, :], ALU.add).then_inc(S["ya"], 1)
                        dve.wait_ge(S["ya"], 1 + n)
                        dve.wait_ge(S["x2_out"], 1 + TPB * i)
                        dve.tensor_tensor(t2[:, t, :], t1[:, t, :], tile(x_sb, i, t), ALU.add).then_inc(S["x2"], 1)
                        dve.wait_ge(S["x2"], 1 + n)
                        dve.bn_stats(st[:, t, :], t2[:, t, :]).then_inc(S["st"], 1)
                    dve.wait_ge(S["st"], TPB * (i + 1))
                    variance_and_mean(dve, S, st, mom, ve, i)
                    dve.wait_ge(S["rstd"], i + 1)
                    for t in range(TPB):
                        dve.tensor_scalar(t1[:, t, :], t2[:, t, :], mom[:, 0, t:t + 1], rstd[:, t:t + 1],
                                          ALU.subtract, ALU.mult).then_inc(S["x3"], 1)
                    dve.wait_ge(S["lg"], 1 + i + 1)
                    dve.tensor_copy(lg[:, bass.ds(i * (TPB * E), TPB * E)], lb[:, 0:TPB * E]).then_inc(S["lg_out"], 1)
                dve.wait_ge(S["lg_out"], 1 + NBLK)


def route(nc, sems, c, x3, lg, cw, gi, zero, disp):
    with ExitStack() as ctx:
        sb, pb = memory(ctx, nc, "r")
        S = sems["r"]
        m8, i8 = sb("m8", [P, NT, 8]), sb("i8", [P, NT, 8], U32)
        ef = sb("ef", [P, K, NT])
        oh = sb("oh", [P, K, NT, E])
        both, incl, excl = sb("both", [P, NT, E]), sb("incl", [P, NT, E]), sb("excl", [P, NT, E])
        rk, tmp = sb("rk", [P, NT, E]), sb("tmp", [P, K, NT, E])
        rank, keep, base = sb("rank", [P, K, NT]), sb("keep", [P, K, NT]), sb("base", [P, K, NT])
        sf, gf, far = sb("sf", [P, K, NT]), sb("gf", [P, K, NT]), sb("far", [P, K, NT])
        si = sb("si", [P, K, NT], U32)
        d, ex, one = sb("d", [P, NT]), sb("ex", [P, NT]), sb("one", [P, NT])
        wr = sb("wr", [P, K, NT])
        rb = pb("rb", [P, NT * E])

        with nc.Block() as block:

            @block.sync
            def _(sp):
                for e in range(E):
                    sp.dma_start(disp[e * SLOTS:(e + 1) * SLOTS, :].rearrange("(p t) d -> p t d", t=ST),
                                 zero[:, :, :]).then_inc(S["zeroed"], 16)

            @block.scalar
            def _(act):
                act.wait_ge(S["d"], 1)
                act.activation(ex[:, :], d[:, :], ACT.Exp).then_inc(S["ex"], 1)

            @block.tensor
            def _(pe):
                pe.wait_ge(S["excl"], 1)
                pe.matmul(rb[:, :], c["before"][:, :], both[:, :, :].rearrange("p t e -> p (t e)"), start=True, stop=False)
                pe.matmul(rb[:, :], c["ones"][:, :], excl[:, :, :].rearrange("p t e -> p (t e)"), start=False, stop=True)\
                    .then_inc(S["rb"], 1)

            @block.gpsimd
            def _(pool):
                pool.wait_ge(S["zeroed"], 16 * E)
                pool.wait_ge(S["si"], 1)
                for t in range(NT):
                    for k in range(K):
                        pool.indirect_dma_start(
                            out=disp, out_offset=bass.IndirectOffsetOnAxis(ap=si[:, k, t:t + 1], axis=0),
                            in_=x3[:, t * D:(t + 1) * D], in_offset=None,
                            bounds_check=E * SLOTS - 1, oob_is_err=False).then_inc(S["sent"], 16)
                pool.wait_ge(S["sent"], 16 * K * NT)

            @block.vector
            def _(dve):
                n = [0]

                def chain(ins):
                    n[0] += 1
                    ins.then_inc(S["step"], 1)
                    dve.wait_ge(S["step"], n[0])

                for t in range(NT):
                    dve.max(m8[:, t, :], lg[:, t * E:(t + 1) * E]).then_inc(S["m8"], 1)
                for t in range(NT):
                    dve.wait_ge(S["m8"], t + 1)
                    dve.max_index(i8[:, t, :], m8[:, t, :], lg[:, t * E:(t + 1) * E]).then_inc(S["i8"], 1)
                dve.tensor_tensor(d[:, :], m8[:, :, 1], m8[:, :, 0], ALU.subtract).then_inc(S["d"], 1)
                dve.wait_ge(S["i8"], NT)
                for k in range(K):
                    chain(dve.tensor_copy(ef[:, k, :], i8[:, :, k]))
                    chain(dve.tensor_tensor(oh[:, k, :, :], ef[:, k, :].unsqueeze(2).to_broadcast([P, NT, E]),
                                            c["iota"][:, :].unsqueeze(1).to_broadcast([P, NT, E]), ALU.is_equal))
                chain(dve.tensor_tensor(both[:, :, :], oh[:, 0, :, :], oh[:, 1, :, :], ALU.add))
                for e in range(E):
                    chain(dve.tensor_tensor_scan(incl[:, :, e], both[:, :, e], both[:, :, e], 0.0, ALU.add, ALU.bypass))
                dve.tensor_tensor(excl[:, :, :], incl[:, :, :], both[:, :, :], ALU.subtract).then_inc(S["excl"], 1)
                dve.wait_ge(S["ex"], 1)
                chain(dve.tensor_scalar(one[:, :], ex[:, :], 1.0, None, ALU.add))
                chain(dve.reciprocal(wr[:, 0, :], one[:, :]))
                chain(dve.tensor_tensor(wr[:, 1, :], ex[:, :], wr[:, 0, :], ALU.mult))
                dve.wait_ge(S["rb"], 1)
                chain(dve.tensor_copy(rk[:, :, :].rearrange("p t e -> p (t e)"), rb[:, :]))
                for k in range(K):
                    chain(dve.tensor_tensor(tmp[:, k, :, :], rk[:, :, :], oh[:, k, :, :], ALU.mult))
                    chain(dve.tensor_reduce(rank[:, k, :], tmp[:, k, :, :], AX.X, ALU.add))
                chain(dve.tensor_scalar(keep[:, :, :], rank[:, :, :], float(CAP), None, ALU.is_lt))
                chain(dve.tensor_scalar(base[:, :, :], ef[:, :, :], float(SLOTS), None, ALU.mult))
                chain(dve.scalar_tensor_tensor(gf[:, :, :], rank[:, :, :], float(CAP - 1), base[:, :, :], ALU.min, ALU.add))
                chain(dve.tensor_scalar(far[:, :, :], keep[:, :, :], -float(FAR), float(FAR), ALU.mult, ALU.add))
                chain(dve.tensor_tensor(sf[:, :, :], far[:, :, :], gf[:, :, :], ALU.add))
                dve.tensor_copy(si[:, :, :], sf[:, :, :]).then_inc(S["si"], 1)
                chain(dve.tensor_copy(gi[:, :, :], gf[:, :, :]))
                chain(dve.tensor_tensor(cw[:, :, :], wr[:, :, :], keep[:, :, :], ALU.mult))


def experts(nc, sems, c, disp, ybuf, w1, w2):
    W1 = DC * FF
    W2 = FC * D
    with ExitStack() as ctx:
        sb, pb = memory(ctx, nc, "f")
        S = sems["f"]
        s1, s2 = sb("s1", [P, W1]), sb("s2", [P, W2])
        w1h, w1l = sb("w1h", [P, W1], F32R), sb("w1l", [P, W1], F32R)
        w2h, w2l = sb("w2h", [P, W2], F32R), sb("w2l", [P, W2], F32R)
        rows = sb("rows", [SP_, ST, D])
        xh, xl = sb("xh", [P, DC, SLOTS], F32R), sb("xl", [P, DC, SLOTS], F32R)
        th, v = sb("th", [P, 2, HALF]), sb("v", [P, 2, HALF])
        hh, hl = sb("hh", [P, FC, SLOTS], F32R), sb("hl", [P, FC, SLOTS], F32R)
        y = sb("y", [SP_, ST, D])
        tb = [pb(f"tb{n}", [P, 512]) for n in range(2)]
        hb = [pb(f"hb{n}", [P, 512]) for n in range(3)]
        yb = [pb(f"yb{n}", [P, 512]) for n in range(3)]
        HU = 2 * FC

        with nc.Block() as block:

            @block.sync
            def _(sp):
                with sp.Fori(0, E) as e:
                    sp.wait_ge(S["rows_used"], 1 + e)
                    sp.dma_start(rows[:, :, :], disp[bass.ds(e * SLOTS, SLOTS), :].rearrange("(p t) d -> p t d", t=ST))\
                        .then_inc(S["rows"], 16)
                    sp.wait_ge(S["w1l"], 1 + e)
                    sp.dma_start(s1[:, :].rearrange("p (k f) -> p k f", k=DC),
                                 w1[bass.ds(e * D, D), :].rearrange("(k p) f -> p k f", p=P)).then_inc(S["s1"], 16)
                    sp.wait_ge(S["w2l"], 1 + e)
                    sp.dma_start(s2[:, :].rearrange("p (k d) -> p k d", k=FC),
                                 w2[bass.ds(e * FF, FF), :].rearrange("(k p) d -> p k d", p=P)).then_inc(S["s2"], 16)

            @block.gpsimd
            def _(pool):
                with pool.Fori(0, E) as e:
                    pool.wait_ge(S["w1h"], e + 1)
                    pool.wait_ge(S["s1"], 16 * (e + 1))
                    pool.tensor_tensor(w1l[:, :], s1[:, :], w1h[:, :].bitcast(F32), ALU.subtract).then_inc(S["w1l"], 1)
                    pool.wait_ge(S["w2h"], e + 1)
                    pool.wait_ge(S["s2"], 16 * (e + 1))
                    pool.tensor_tensor(w2l[:, :], s2[:, :], w2h[:, :].bitcast(F32), ALU.subtract).then_inc(S["w2l"], 1)

            @block.scalar
            def _(act):
                with act.Fori(0, E) as e:
                    act.wait_ge(S["s1"], 16 * (e + 1))
                    act.wait_ge(S["h"], 1 + HU * e)
                    act.activation(w1h[:, :], s1[:, :], ACT.Copy).then_inc(S["w1h"], 1)
                    for n in range(2 * DC):
                        k, f = n % DC, n // DC
                        act.wait_ge(S["T"], 2 * DC * e + n + 1)
                        act.activation(xh[:, k, f * HALF:(f + 1) * HALF], tb[n % 2][:, 0:HALF], ACT.Copy)\
                            .then_inc(S["xh"], 1)
                    act.wait_ge(S["s2"], 16 * (e + 1))
                    act.wait_ge(S["y"], 1 + ST * e)
                    act.activation(w2h[:, :], s2[:, :], ACT.Copy).then_inc(S["w2h"], 1)
                    for u in range(HU + 1):
                        if u < HU:
                            act.wait_ge(S["h"], 1 + HU * e + u + 1)
                            act.wait_ge(S["v"], 1 + HU * e + max(u - 1, 0))
                            act.activation(th[:, u % 2, :], hb[u % 3][:, 0:HALF], ACT.Tanh, scale=0.5).then_inc(S["th"], 1)
                        if u >= 1:
                            f, s = divmod(u - 1, 2)
                            act.wait_ge(S["v"], 1 + HU * e + u)
                            act.activation(hh[:, f, s * HALF:(s + 1) * HALF], v[:, (u - 1) % 2, :], ACT.Copy, scale=0.5)\
                                .then_inc(S["hh"], 1)
                    for t in range(ST):
                        act.wait_ge(S["y"], 1 + ST * e + t + 1)
                        act.wait_ge(S["stored"], 1 + 16 * e)
                        act.activation(y[:, t, :], yb[t % 3][0:SP_, 0:D], ACT.Copy).then_inc(S["y_out"], 1)
                    act.wait_ge(S["y_out"], 1 + ST * (e + 1))
                    act.dma_start(ybuf[bass.ds(e * SLOTS, SLOTS), :].rearrange("(p t) d -> p t d", t=ST), y[:, :, :])\
                        .then_inc(S["stored"], 16)
                act.wait_ge(S["stored"], 1 + 16 * E)

            @block.tensor
            def _(pe):
                with pe.Fori(0, E) as e:
                    pe.wait_ge(S["rows"], 16 * (e + 1))
                    for n in range(2 * DC):
                        k, f = n % DC, n // DC
                        pe.wait_ge(S["xl"], 1 + 2 * DC * e + max(n - 1, 0))
                        for t in range(3):
                            mm = pe.transpose(tb[n % 2][:, t * SP_:(t + 1) * SP_], rows[:, 3 * f + t, k * P:(k + 1) * P],
                                              c["ident"][0:SP_, 0:SP_])
                        mm.then_inc(S["T"], 1)
                    pe.wait_ge(S["xh"], 2 * DC * (e + 1))
                    pe.wait_ge(S["xl"], 1 + 2 * DC * (e + 1))
                    pe.wait_ge(S["w1l"], 1 + e + 1)
                    for u in range(HU):
                        f, s = divmod(u, 2)
                        pe.wait_ge(S["v"], 1 + HU * e + max(u - 2, 0))
                        split_product(pe, hb[u % 3][:, 0:HALF],
                                      [((w1h[:, k * FF + f * P:k * FF + (f + 1) * P], w1l[:, k * FF + f * P:k * FF + (f + 1) * P]),
                                        (xh[:, k, s * HALF:(s + 1) * HALF], xl[:, k, s * HALF:(s + 1) * HALF]))
                                       for k in range(DC)]).then_inc(S["h"], 1)
                    pe.wait_ge(S["w2l"], 1 + e + 1)
                    pe.wait_ge(S["hh"], 1 + HU * (e + 1))
                    pe.wait_ge(S["hl"], 1 + HU * (e + 1))
                    for t in range(ST):
                        pe.wait_ge(S["y_out"], 1 + ST * e + max(t - 2, 0))
                        s = slice(t * SP_, (t + 1) * SP_)
                        split_product(pe, yb[t % 3][0:SP_, 0:D],
                                      [((hh[:, f, s], hl[:, f, s]), (w2h[:, f * D:(f + 1) * D], w2l[:, f * D:(f + 1) * D]))
                                       for f in range(FC)]).then_inc(S["y"], 1)

            @block.vector
            def _(dve):
                with dve.Fori(0, E) as e:
                    for n in range(2 * DC):
                        k, f = n % DC, n // DC
                        s = slice(f * HALF, (f + 1) * HALF)
                        dve.wait_ge(S["xh"], 2 * DC * e + n + 1)
                        ins = dve.tensor_tensor(xl[:, k, s], tb[n % 2][:, 0:HALF], xh[:, k, s].bitcast(F32), ALU.subtract)
                        ins.then_inc(S["xl"], 1)
                    dve.wait_ge(S["T"], 2 * DC * (e + 1))
                    dve.sem_inc(S["rows_used"], 1)
                    for u in range(HU + 1):
                        if u < HU:
                            dve.wait_ge(S["th"], HU * e + u + 1)
                            dve.wait_ge(S["hl"], 1 + HU * e + max(u - 1, 0))
                            dve.scalar_tensor_tensor(v[:, u % 2, :], th[:, u % 2, :], 1.0, hb[u % 3][:, 0:HALF],
                                                     ALU.add, ALU.mult).then_inc(S["v"], 1)
                        if u >= 1:
                            f, s = divmod(u - 1, 2)
                            s = slice(s * HALF, (s + 1) * HALF)
                            dve.wait_ge(S["hh"], 1 + HU * e + u)
                            dve.scalar_tensor_tensor(hl[:, f, s], v[:, (u - 1) % 2, :], 0.5, hh[:, f, s].bitcast(F32),
                                                     ALU.mult, ALU.subtract).then_inc(S["hl"], 1)


def combine(nc, sems, x_sb, x3, cw, gi, ybuf, out):
    with ExitStack() as ctx:
        sb, _ = memory(ctx, nc, "o")
        S = sems["o"]
        got = sb("got", [P, NT * K * D])
        acc = sb("acc", [P, NT * D])
        with nc.Block() as block:

            @block.gpsimd
            def _(pool):
                for t in range(NT):
                    for k in range(K):
                        at = (t * K + k) * D
                        pool.indirect_dma_start(
                            out=got[:, at:at + D], out_offset=None, in_=ybuf,
                            in_offset=bass.IndirectOffsetOnAxis(ap=gi[:, k, t:t + 1], axis=0),
                            bounds_check=E * SLOTS - 1, oob_is_err=False).then_inc(S[f"got{t // TPB}"], 16)

            @block.vector
            def _(dve):
                for t in range(NT):
                    s, g = slice(t * D, (t + 1) * D), t * K * D
                    dve.wait_ge(S[f"got{t // TPB}"], 16 * K * TPB)
                    dve.scalar_tensor_tensor(acc[:, s], got[:, g:g + D], cw[:, 0, t:t + 1], x3[:, s], ALU.mult, ALU.add)\
                        .then_inc(S["a1"], 1)
                    dve.wait_ge(S["a1"], t + 1)
                    dve.scalar_tensor_tensor(acc[:, s], got[:, g + D:g + 2 * D], cw[:, 1, t:t + 1], acc[:, s],
                                             ALU.mult, ALU.add).then_inc(S["a2"], 1)
                    dve.wait_ge(S["a2"], t + 1)
                    dve.tensor_tensor(acc[:, s], acc[:, s], x_sb[:, s], ALU.add).then_inc(S["a3"], 1)

            @block.sync
            def _(sp):
                for i in range(NBLK):
                    sp.wait_ge(S["a3"], TPB * (i + 1))
                    sp.dma_start(out[i * BLK:(i + 1) * BLK, :].rearrange("(t p) d -> p t d", p=P),
                                 acc[:, i * TPB * D:(i + 1) * TPB * D].rearrange("p (t d) -> p t d", d=D))\
                        .then_inc(S["stored"], 16)
                sp.wait_ge(S["stored"], 16 * NBLK)


def build(nc, a, out, phases="MQWFC"):
    with ExitStack() as ctx:
        sems = {phase: Sems(ctx, nc, phase) for phase in "cmqawrfo"}
        sb, _ = memory(ctx, nc, "g")
        x_sb = sb("x", [P, NT * D])
        c = constants(nc, ctx, sems)
        w = {n: a["L0_attn_" + n] for n in MIX}
        vec = {n: a["L0_attn_" + n] for n in ("conv_w", "conv_b", "dl_b", "A_b", "B_b", "C_b", "D_b")}
        mixer(nc, sems, c, x_sb, a["x"], w, vec)
        if "Q" in phases:
            with ExitStack() as keep:
                sb2, _ = memory(keep, nc, "h")
                x3, lg = sb("x3", [P, NT * D]), sb("lg", [P, NT * E])
                woh, wol = sb2("woh", [P, DC * D], F32R), sb2("wol", [P, DC * D], F32R)
                bo, o_sb = sb2("bo", [P, D]), sb2("o", [P, NT * D])
                with ExitStack() as qkv:
                    sb3, _ = memory(qkv, nc, "i")
                    qt, kt = sb3("qt", [P, DC * N]), sb3("kt", [P, DC * N])
                    vs = sb3("vs", [P, NT * HEADS * 3 * VW], BF16)
                    wx = {n: a["L0_xattn_" + n] for n in ("WQ", "WK", "WV", "WO", "bQ", "bK", "bV", "bO")}
                    projections(nc, sems, c, x_sb, a["ctx_1024"], wx, wx, qt, kt, vs, woh, wol, bo)
                    attention(nc, sems, c, qt, kt, vs, o_sb)
                output_and_router(nc, sems, c, x_sb, o_sb, x3, lg, woh, wol, bo, a["L0_ffn_router_w"])
        if "F" in phases:
            cw, gi = sb("cw", [P, K, NT]), sb("gi", [P, K, NT], U32)
            disp = nc.dram_tensor("disp", (E * SLOTS, D), F32).ap()
            ybuf = nc.dram_tensor("ybuf", (E * SLOTS, D), F32).ap()
            route(nc, sems, c, x3, lg, cw, gi, c["zero"], disp)
            experts(nc, sems, c, disp, ybuf, a["L0_ffn_w1"], a["L0_ffn_w2"])
            combine(nc, sems, x_sb, x3, cw, gi, ybuf, out)
            return
        done = ctx.enter_context(nc.semaphore("done"))
        with nc.Block() as block:
            @block.sync
            def _(sp):
                sp.dma_start(out.rearrange("(t p) d -> p t d", p=P),
                             x_sb[:, :].rearrange("p (t d) -> p t d", d=D)).then_inc(done, 16)
                sp.wait_ge(done, 16)


def layout(inputs):
    import numpy as np
    out = {}
    for name, v in inputs.items():
        v = np.asarray(v)
        short = name.replace("L0_attn_", "")
        if name.startswith("L0_attn_") and short in MIX or name == "L0_ffn_router_w":
            v = v.T
        elif short == "conv_w":
            v = v.reshape(D, 3)
        elif name in ("L0_xattn_bV", "L0_xattn_bO"):
            v = v.reshape(1, D)
        elif v.ndim == 1:
            v = v.reshape(-1, P).T
        elif v.ndim == 3:
            v = v.reshape(-1, v.shape[-1])
        out[name] = np.ascontiguousarray(v)
    return out


_OUT = (B, L, D)


def kernel(**inputs):
    import numpy as _np
    import concourse.bacc as _bacc
    from concourse import mybir as _mybir
    from concourse.bass_utils import run_bass_kernel_spmd as _run

    nc = _bacc.Bacc("TRN2", target_bir_lowering=False, num_devices=1)
    arrays = {f"in_{n}": v for n, v in layout(inputs).items()}
    args = {n[3:]: nc.dram_tensor(n, v.shape, _mybir.dt.from_np(v.dtype), kind="ExternalInput").ap()
            for n, v in arrays.items()}
    out = nc.dram_tensor("out", (N, D), F32, kind="ExternalOutput").ap()
    build(nc, args, out)
    r = _run(nc, [arrays], core_ids=[0])
    return _np.asarray(r.results[0]["out"]).reshape(_OUT)
```

```python
from contextlib import ExitStack

import concourse.bass as bass
from concourse import mybir

F32 = mybir.dt.float32
F32R = mybir.dt.float32r
BF16 = mybir.dt.bfloat16
F16 = mybir.dt.float16
U32 = mybir.dt.uint32
ALU = mybir.AluOpType
ACT = mybir.ActivationFunctionType
AX = mybir.AxisListType

P = 128
B, L, D = 8, 256, 256
N = B * L
DC = D // P
NT = N // P
BLK = 512
TPB = BLK // P
NBLK = N // BLK
HID = 512
HC = HID // P
HEADS, HD = 16, 16
SCALE = 1.0 / HD ** 0.5
E, K, FF = 8, 2, 1024
FC = FF // P
CAP = int(1.25 * N * K / E) + 1
ST = 6
SP_ = -(-CAP // (ST * 4)) * 4
SLOTS = ST * SP_
HALF = SLOTS // 2
FAR = 1 << 20
EPS = 1e-5
NEG = -1e30
VW = HD + 1

MIX = {}
_at = 0
for _name, _kc, _out in (("w1", DC, D), ("w2", DC, D), ("w3", DC, D), ("D_w", DC, D),
                         ("dl_w", DC, HID), ("A_w", DC, HID), ("B_w", DC, HID), ("C_w", HC, D)):
    MIX[_name] = (_at, _kc, _out)
    _at += _kc * _out
MIXW = _at


class Sems:

    def __init__(self, ctx, nc, prefix):
        self.ctx, self.nc, self.prefix, self.made = ctx, nc, prefix, {}

    def __getitem__(self, name):
        if name not in self.made:
            self.made[name] = self.ctx.enter_context(self.nc.semaphore(f"{self.prefix}_{name}"))
        return self.made[name]


START_AT_ONE = {
    "m": ("C", "conv", "hl", "w1", "x_out", "zl"),
    "q": ("cT", "k_out", "q", "q_out", "v", "vf", "vr", "xT"),
    "w": ("lg", "lg_out", "ol", "x2", "x2_out", "x3_out", "xT", "xt", "y", "ya"),
    "f": ("T", "h", "hl", "hl_odd", "stored", "v", "w1l", "w2l", "xl", "y", "y_out"),
}


def memory(ctx, nc, prefix):
    def sb(name, shape, dt=F32):
        return ctx.enter_context(nc.sbuf_tensor(f"{prefix}_{name}", shape, dt))

    def pb(name, shape, dt=F32):
        return ctx.enter_context(nc.psum_tensor(f"{prefix}_{name}", shape, dt))

    return sb, pb


def split_product(pe, out, parts, first=True, last=True):
    n = 0
    for (lh, ll), (rh, rl) in parts:
        for a, b in ((lh, rh), (lh, rl), (ll, rh)):
            mm = pe.matmul(out, a, b, start=first and n == 0, stop=last and n == 3 * len(parts) - 1)
            n += 1
    return mm


def variance_and_mean(dve, S, st, mom, ve, i):
    dve.tensor_tensor(mom[:, 1, :], st[:, :, 1], st[:, :, 4], ALU.add).then_inc(S["mom"], 1)
    dve.tensor_tensor(mom[:, 2, :], st[:, :, 1], st[:, :, 4], ALU.subtract).then_inc(S["mom"], 1)
    dve.tensor_tensor(mom[:, 3, :], st[:, :, 2], st[:, :, 5], ALU.add).then_inc(S["mom"], 1)
    dve.wait_ge(S["mom"], 5 * i + 3)
    dve.tensor_scalar(mom[:, 0, :], mom[:, 1, :], 0.5, None, ALU.mult).then_inc(S["mean"], 1)
    dve.scalar_tensor_tensor(mom[:, 2, :], mom[:, 2, :], 0.25, mom[:, 2, :], ALU.mult, ALU.mult).then_inc(S["mom"], 1)
    dve.tensor_scalar(mom[:, 3, :], mom[:, 3, :], 1.0 / D, EPS, ALU.mult, ALU.add).then_inc(S["mom"], 1)
    dve.wait_ge(S["mom"], 5 * i + 5)
    dve.wait_ge(S["mean"], i + 1)
    dve.tensor_tensor(ve[:, :], mom[:, 2, :], mom[:, 3, :], ALU.add).then_inc(S["ve"], 1)


def constants(nc, ctx, sems):
    sb, _ = memory(ctx, nc, "c")
    S = sems["c"]
    c = {
        "ident": sb("ident", [P, P]), "identb": sb("identb", [P, P], BF16),
        "place": sb("place", [P, DC, D], F32R),
        "mask": sb("mask", [P, P], BF16), "head": sb("head", [P, P // HD]),
        "ones": sb("ones", [P, P]), "before": sb("before", [P, P]),
        "zero": sb("zeros", [SP_, ST, D]),
        "mhalf": sb("mhalf", [P, TPB]), "iota": sb("iota", [P, E]),
    }
    place32 = sb("place32", [P, DC, D])
    with nc.Block() as block:

        @block.sync
        def _(sp):
            for phase, names in START_AT_ONE.items():
                for name in names:
                    sp.sem_inc(sems[phase][name], 1)

        @block.gpsimd
        def _(pool):
            pool.memset(c["ident"][:, :], 0.0).then_inc(S["zero"], 1)
            pool.memset(c["identb"][:, :], 0.0).then_inc(S["zero"], 1)
            pool.memset(place32[:, :, :], 0.0).then_inc(S["zero"], 1)
            pool.memset(c["mask"][:, :], 0.0).then_inc(S["zero"], 1)
            pool.memset(c["head"][:, :], 1.0).then_inc(S["zero"], 1)
            pool.memset(c["ones"][:, :], 1.0).then_inc(S["zero"], 1)
            pool.memset(c["before"][:, :], 1.0).then_inc(S["zero"], 1)
            pool.memset(c["mhalf"][:, :], -0.5).then_inc(S["zero"], 1)
            pool.memset(c["zero"][:, :, :], 0.0).then_inc(S["zero"], 1)
            for e in range(E):
                pool.memset(c["iota"][:, e:e + 1], float(e)).then_inc(S["zero"], 1)
            pool.wait_ge(S["zero"], 9 + E)
            for m in (c["ident"], c["identb"]):
                pool.affine_select(out=m[:, :], in_=m[:, :], compare_op=ALU.not_equal, fill=1.0, base=0,
                                   pattern=[[-1, P]], channel_multiplier=1).then_inc(S["made"], 1)
            for k in range(DC):
                v = place32[:, k, k * P:(k + 1) * P]
                pool.affine_select(out=v, in_=v, compare_op=ALU.not_equal, fill=1.0, base=0,
                                   pattern=[[-1, P]], channel_multiplier=1).then_inc(S["made"], 1)
            pool.affine_select(out=c["mask"][:, :], in_=c["mask"][:, :], compare_op=ALU.is_ge, fill=NEG,
                               base=0, pattern=[[-1, P]], channel_multiplier=1).then_inc(S["made"], 1)
            pool.affine_select(out=c["before"][:, :], in_=c["before"][:, :], compare_op=ALU.is_ge,
                               fill=0.0, base=-1, pattern=[[1, P]], channel_multiplier=-1).then_inc(S["made"], 1)
            pool.affine_select(out=c["head"][:, :], in_=c["head"][:, :], compare_op=ALU.is_ge, fill=0.0,
                               base=0, pattern=[[-HD, P // HD]], channel_multiplier=1).then_inc(S["head"], 1)
            pool.wait_ge(S["head"], 1)
            pool.affine_select(out=c["head"][:, :], in_=c["head"][:, :], compare_op=ALU.is_ge, fill=0.0,
                               base=HD - 1, pattern=[[HD, P // HD]], channel_multiplier=-1).then_inc(S["made"], 1)

        @block.vector
        def _(dve):
            dve.wait_ge(S["made"], 4)
            dve.tensor_copy(c["place"][:, :, :], place32[:, :, :]).then_inc(S["made"], 1)
            dve.wait_ge(S["made"], 8)

    return c


def mixer(nc, sems, c, x_sb, x, w, vec):
    with ExitStack() as ctx:
        sb, pb = memory(ctx, nc, "m")
        S = sems["m"]
        wst = sb("wst", [P, MIXW])
        wh, wl = sb("wh", [P, MIXW], F32R), sb("wl", [P, MIXW], F32R)
        cw, cb = sb("cw", [P, DC, 3]), sb("cb", [P, DC])
        dlb, Ab, Bb = sb("dlb", [P, HC]), sb("Ab", [P, HC]), sb("Bb", [P, HC])
        Cb, Db, CDb = sb("Cb", [P, DC]), sb("Db", [P, DC]), sb("CDb", [P, DC])
        xin = sb("xin", [P, TPB, D])
        xn = sb("xn", [P, TPB, D])
        st, mom = sb("st", [P, TPB, 6]), sb("mom", [P, 4, TPB])
        ve, rstd = sb("ve", [P, TPB]), sb("rstd", [P, TPB])
        xh, xl = sb("xh", [P, DC, BLK], F32R), sb("xl", [P, DC, BLK], F32R)
        ypad = sb("ypad", [P, DC, 2, L + 2])
        cv, th = sb("cv", [P, DC, BLK]), sb("th", [P, DC, BLK])
        sh, sl = sb("sh", [P, DC, BLK], F32R), sb("sl", [P, DC, BLK], F32R)
        e, a, hs = sb("e", [P, HC, BLK]), sb("a", [P, HC, BLK]), sb("hs", [P, HC, BLK])
        hh, hl = sb("hh", [P, HC, BLK], F32R), sb("hl", [P, HC, BLK], F32R)
        ssm = sb("ssm", [P, DC, BLK])
        banks = [pb(f"bank{n}", [P, BLK]) for n in range(8)]

        def weights(name, k, m0, m):
            at, _, out = MIX[name]
            s = slice(at + k * out + m0, at + k * out + m0 + m)
            return wh[:, s], wl[:, s]

        with nc.Block() as block:

            @block.sync
            def _(sp):
                for name, (at, kc, out) in MIX.items():
                    sp.dma_start(wst[:, at:at + kc * out].rearrange("p (k o) -> p k o", k=kc),
                                 w[name].rearrange("(k p) o -> p k o", p=P)).then_inc(S["w_in"], 16)
                small = ((cw, vec["conv_w"].rearrange("(k p) t -> p k t", p=P)),
                         (cb, vec["conv_b"]),
                         (dlb, vec["dl_b"]),
                         (Ab, vec["A_b"]),
                         (Bb, vec["B_b"]),
                         (Cb, vec["C_b"]),
                         (Db, vec["D_b"]))
                for dst, src in small:
                    sp.dma_start(dst[:], src).then_inc(S["v_in"], 16)
                with sp.Fori(0, NBLK) as i:
                    sp.wait_ge(S["x_out"], 1 + TPB * i)
                    sp.dma_start(xin[:, :, :], x[bass.ds(i * BLK, BLK), :].rearrange("(t p) d -> p t d", p=P))\
                        .then_inc(S["x_in"], 16)

            @block.gpsimd
            def _(pool):
                pool.memset(ypad[:, :, :, :], 0.0).then_inc(S["pad"], 1)
                pool.wait_ge(S["w_in"], 16 * len(MIX))
                pool.wait_ge(S["wh"], 1)
                pool.tensor_tensor(wl[:, :], wst[:, :], wh[:, :].bitcast(F32), ALU.subtract).then_inc(S["wl"], 1)
                with pool.Fori(0, NBLK) as i:
                    pool.wait_ge(S["ve"], i + 1)
                    pool.tensor_tensor(rstd[:, :], ve[:, :], c["mhalf"][:, :], ALU.pow).then_inc(S["rstd"], 1)
                    for m in range(HC):
                        pool.wait_ge(S["hh"], HC * i + m + 1)
                        pool.wait_ge(S["C"], 1 + DC * i)
                        pool.tensor_tensor(hl[:, m, :], hs[:, m, :], hh[:, m, :].bitcast(F32), ALU.subtract)\
                            .then_inc(S["hl"], 1)

            @block.scalar
            def _(act):
                act.wait_ge(S["w_in"], 16 * len(MIX))
                act.activation(wh[:, :], wst[:, :], ACT.Copy).then_inc(S["wh"], 1)
                act.wait_ge(S["pad"], 1)
                act.wait_ge(S["v_in"], 16 * 7)
                with act.Fori(0, NBLK) as i:
                    for k in range(DC):
                        act.wait_ge(S["xT"], DC * i + k + 1)
                        act.wait_ge(S["w1"], 1 + DC * i)
                        act.activation(xh[:, k, :], banks[k][:, :], ACT.Copy).then_inc(S["xh"], 1)
                    for m in range(DC):
                        act.wait_ge(S["w1"], 1 + DC * i + m + 1)
                        act.wait_ge(S["conv"], 1 + DC * i)
                        act.activation(ypad[:, m, :, 1:L + 1],
                                       banks[2 + m][:, :].rearrange("p (b l) -> p b l", b=2),
                                       ACT.Copy).then_inc(S["y"], 1)
                    for m in range(DC):
                        act.wait_ge(S["conv"], 1 + DC * i + m + 1)
                        act.activation(th[:, m, :], cv[:, m, :], ACT.Tanh, scale=0.5).then_inc(S["th"], 1)
                    for m in range(DC):
                        act.wait_ge(S["silu"], DC * i + m + 1)
                        act.wait_ge(S["C"], 1 + DC * i)
                        act.activation(sh[:, m, :], cv[:, m, :], ACT.Copy, scale=0.5).then_inc(S["sh"], 1)
                    for m in range(HC):
                        act.wait_ge(S["dmin"], HC * i + m + 1)
                        act.activation(e[:, m, :], e[:, m, :], ACT.Exp).then_inc(S["dexp"], 1)
                    for m in range(HC):
                        act.wait_ge(S["dexp"], HC * i + m + 1)
                        act.activation(e[:, m, :], e[:, m, :], ACT.Ln, bias=1.0).then_inc(S["dln"], 1)
                    for m in range(HC):
                        act.wait_ge(S["dA"], HC * i + m + 1)
                        act.activation(e[:, m, :], e[:, m, :], ACT.Exp, scale=-1.0).then_inc(S["abar"], 1)
                    for m in range(HC):
                        act.wait_ge(S["h"], HC * i + m + 1)
                        act.wait_ge(S["C"], 1 + DC * i)
                        act.activation(hh[:, m, :], hs[:, m, :], ACT.Copy).then_inc(S["hh"], 1)
                    for m in range(DC):
                        act.wait_ge(S["C"], 1 + DC * i + m + 1)
                        act.wait_ge(S["bias"], 1)
                        act.activation(ssm[:, m, :], banks[4 + m][:, :], ACT.Identity, bias=CDb[:, m:m + 1])\
                            .then_inc(S["ssm"], 1)
                        act.wait_ge(S["ssm"], DC * i + m + 1)
                        act.activation(xh[:, m, :], ssm[:, m, :], ACT.Copy).then_inc(S["ssmh"], 1)
                    for m in range(DC):
                        act.wait_ge(S["w2"], DC * i + m + 1)
                        act.activation(th[:, m, :], banks[6 + m][:, :], ACT.Tanh, scale=0.5).then_inc(S["th2"], 1)
                    for m in range(DC):
                        act.wait_ge(S["z"], DC * i + m + 1)
                        act.activation(sh[:, m, :], cv[:, m, :], ACT.Copy, scale=0.5).then_inc(S["zh"], 1)

            @block.tensor
            def _(pe):
                pe.wait_ge(S["wl"], 1)
                with pe.Fori(0, NBLK) as i:
                    for k in range(DC):
                        pe.wait_ge(S["x_out"], 1 + TPB * i)
                        for t in range(TPB):
                            pe.wait_ge(S["xn"], TPB * i + t + 1)
                            mm = pe.transpose(banks[k][:, t * P:(t + 1) * P], xn[:, t, k * P:(k + 1) * P],
                                              c["ident"][:, :])
                        mm.then_inc(S["xT"], 1)
                    pe.wait_ge(S["xh"], DC * (i + 1))
                    pe.wait_ge(S["xl"], DC * (i + 1))
                    for m in range(DC):
                        split_product(pe, banks[2 + m][:, :],
                                      [(weights("w1", k, m * P, P), (xh[:, k, :], xl[:, k, :])) for k in range(DC)])\
                            .then_inc(S["w1"], 1)
                    xs = [(sh[:, k, :], sl[:, k, :]) for k in range(DC)]
                    pe.wait_ge(S["sh"], DC * (i + 1))
                    pe.wait_ge(S["sl"], DC * (i + 1))
                    for m in range(HC):
                        split_product(pe, banks[m][:, :],
                                      [(weights("dl_w", k, m * P, P), xs[k]) for k in range(DC)]).then_inc(S["dl"], 1)
                    for m in range(HC):
                        split_product(pe, banks[4 + m][:, :],
                                      [(weights("A_w", k, m * P, P), xs[k]) for k in range(DC)]).then_inc(S["A"], 1)
                    for m in range(HC):
                        pe.wait_ge(S["delta"], HC * i + m + 1)
                        split_product(pe, banks[m][:, :],
                                      [(weights("B_w", k, m * P, P), xs[k]) for k in range(DC)]).then_inc(S["Bx"], 1)
                    pe.wait_ge(S["hh"], HC * (i + 1))
                    pe.wait_ge(S["hl"], 1 + HC * (i + 1))
                    pe.wait_ge(S["dA"], HC * (i + 1))
                    for m in range(DC):
                        split_product(pe, banks[4 + m][:, :],
                                      [(weights("D_w", k, m * P, P), xs[k]) for k in range(DC)]
                                      + [(weights("C_w", k, m * P, P), (hh[:, k, :], hl[:, k, :])) for k in range(HC)])\
                            .then_inc(S["C"], 1)
                    pe.wait_ge(S["ssmh"], DC * (i + 1))
                    pe.wait_ge(S["ssml"], DC * (i + 1))
                    for m in range(DC):
                        split_product(pe, banks[6 + m][:, :],
                                      [(weights("w2", k, m * P, P), (xh[:, k, :], xl[:, k, :])) for k in range(DC)])\
                            .then_inc(S["w2"], 1)
                    pe.wait_ge(S["zh"], DC * (i + 1))
                    pe.wait_ge(S["zl"], 1 + DC * (i + 1))
                    for t in range(TPB):
                        out = banks[t][:, 0:D]
                        tok = slice(t * P, (t + 1) * P)
                        for k in range(DC):
                            pe.matmul(out, xh[:, k, tok], c["place"][:, k, :], start=k == 0, stop=False)
                            pe.matmul(out, xl[:, k, tok], c["place"][:, k, :], start=False, stop=False)
                        split_product(pe, out, [((sh[:, k, tok], sl[:, k, tok]), weights("w3", k, 0, D))
                                                for k in range(DC)], first=False).then_inc(S["w3"], 1)

            @block.vector
            def _(dve):
                dve.wait_ge(S["v_in"], 16 * 7)
                dve.tensor_tensor(CDb[:, :], Cb[:, :], Db[:, :], ALU.add).then_inc(S["bias"], 1)
                dve.wait_ge(S["pad"], 1)
                with dve.Fori(0, NBLK) as i:
                    dve.wait_ge(S["x_in"], 16 * (i + 1))
                    for t in range(TPB):
                        dve.bn_stats(st[:, t, :], xin[:, t, :]).then_inc(S["st"], 1)
                    dve.wait_ge(S["st"], TPB * (i + 1))
                    variance_and_mean(dve, S, st, mom, ve, i)
                    dve.wait_ge(S["rstd"], i + 1)
                    for t in range(TPB):
                        dve.tensor_scalar(xn[:, t, :], xin[:, t, :], mom[:, 0, t:t + 1], rstd[:, t:t + 1],
                                          ALU.subtract, ALU.mult).then_inc(S["xn"], 1)
                    for k in range(DC):
                        dve.wait_ge(S["xh"], DC * i + k + 1)
                        dve.tensor_tensor(xl[:, k, :], banks[k][:, :], xh[:, k, :].bitcast(F32), ALU.subtract)\
                            .then_inc(S["xl"], 1)
                    for m in range(DC):
                        dve.wait_ge(S["y"], DC * i + m + 1)
                        dve.wait_ge(S["zl"], 1 + DC * i)
                        acc = cv[:, m, :].rearrange("p (b l) -> p b l", b=2)
                        dve.tensor_scalar(acc, ypad[:, m, :, 1:L + 1], cw[:, m, 1:2], cb[:, m:m + 1],
                                          ALU.mult, ALU.add).then_inc(S["tap"], 1)
                        dve.wait_ge(S["tap"], 2 * (DC * i + m) + 1)
                        dve.scalar_tensor_tensor(acc, ypad[:, m, :, 0:L], cw[:, m, 0:1], acc, ALU.mult, ALU.add)\
                            .then_inc(S["tap"], 1)
                        dve.wait_ge(S["tap"], 2 * (DC * i + m) + 2)
                        dve.scalar_tensor_tensor(acc, ypad[:, m, :, 2:L + 2], cw[:, m, 2:3], acc, ALU.mult, ALU.add)\
                            .then_inc(S["conv"], 1)
                    for m in range(DC):
                        dve.wait_ge(S["th"], DC * i + m + 1)
                        dve.scalar_tensor_tensor(cv[:, m, :], th[:, m, :], 1.0, cv[:, m, :], ALU.add, ALU.mult)\
                            .then_inc(S["silu"], 1)
                    for m in range(DC):
                        dve.wait_ge(S["sh"], DC * i + m + 1)
                        dve.scalar_tensor_tensor(sl[:, m, :], cv[:, m, :], 0.5, sh[:, m, :].bitcast(F32),
                                                 ALU.mult, ALU.subtract).then_inc(S["sl"], 1)
                    for m in range(HC):
                        dve.wait_ge(S["dl"], HC * i + m + 1)
                        dve.tensor_scalar(e[:, m, :], banks[m][:, :], dlb[:, m:m + 1], 40.0, ALU.add, ALU.min)\
                            .then_inc(S["dmin"], 1)
                    for m in range(HC):
                        dve.wait_ge(S["dln"], HC * i + m + 1)
                        dve.scalar_tensor_tensor(e[:, m, :], banks[m][:, :], dlb[:, m:m + 1], e[:, m, :],
                                                 ALU.add, ALU.max).then_inc(S["delta"], 1)
                    for m in range(HC):
                        dve.wait_ge(S["A"], HC * i + m + 1)
                        dve.wait_ge(S["delta"], HC * i + m + 1)
                        dve.scalar_tensor_tensor(e[:, m, :], banks[4 + m][:, :], Ab[:, m:m + 1], e[:, m, :],
                                                 ALU.add, ALU.mult).then_inc(S["dA"], 1)
                    for m in range(HC):
                        dve.wait_ge(S["abar"], HC * i + m + 1)
                        for b in range(2):
                            s = slice(b * L, (b + 1) * L)
                            dve.tensor_tensor_scan(a[:, m, s], e[:, m, s], e[:, m, s], 1.0, ALU.mult, ALU.bypass)\
                                .then_inc(S["acum"], 1)
                        dve.wait_ge(S["acum"], 2 * (HC * i + m + 1))
                        dve.wait_ge(S["Bx"], HC * i + m + 1)
                        dve.scalar_tensor_tensor(a[:, m, :], banks[m][:, :], Bb[:, m:m + 1], a[:, m, :],
                                                 ALU.add, ALU.mult).then_inc(S["Ba"], 1)
                        dve.wait_ge(S["Ba"], HC * i + m + 1)
                        dve.wait_ge(S["hl"], 1 + HC * i)
                        for b in range(2):
                            s = slice(b * L, (b + 1) * L)
                            ins = dve.tensor_tensor_scan(hs[:, m, s], a[:, m, s], a[:, m, s], 0.0, ALU.add, ALU.bypass)
                        ins.then_inc(S["h"], 1)
                    for m in range(DC):
                        dve.wait_ge(S["ssmh"], DC * i + m + 1)
                        dve.tensor_tensor(xl[:, m, :], ssm[:, m, :], xh[:, m, :].bitcast(F32), ALU.subtract)\
                            .then_inc(S["ssml"], 1)
                    for m in range(DC):
                        dve.wait_ge(S["th2"], DC * i + m + 1)
                        dve.scalar_tensor_tensor(cv[:, m, :], th[:, m, :], 1.0, banks[6 + m][:, :], ALU.add, ALU.mult)\
                            .then_inc(S["g"], 1)
                        dve.wait_ge(S["g"], DC * i + m + 1)
                        dve.tensor_tensor(cv[:, m, :], cv[:, m, :], ssm[:, m, :], ALU.mult).then_inc(S["z"], 1)
                    for m in range(DC):
                        dve.wait_ge(S["zh"], DC * i + m + 1)
                        dve.scalar_tensor_tensor(sl[:, m, :], cv[:, m, :], 0.5, sh[:, m, :].bitcast(F32),
                                                 ALU.mult, ALU.subtract).then_inc(S["zl"], 1)
                    for t in range(TPB):
                        dve.wait_ge(S["w3"], TPB * i + t + 1)
                        dve.tensor_tensor(x_sb[:, bass.ds((TPB * i + t) * D, D)],
                                          banks[t][:, 0:D],
                                          xin[:, t, :], ALU.add).then_inc(S["x_out"], 1)
                dve.wait_ge(S["x_out"], 1 + NT)


def load_split(sp_eng, S, wst, parts):
    at = 0
    for src in parts:
        kc, out = src.shape[0] // P, src.shape[1]
        sp_eng.dma_start(wst[:, at:at + kc * out].rearrange("p (k o) -> p k o", k=kc),
                         src.rearrange("(k p) o -> p k o", p=P)).then_inc(S["w_in"], 16)
        at += kc * out


def projections(nc, sems, c, x_sb, ctx_in, w, vec, q_all, k_all, vs, woh, wol, bo):
    with ExitStack() as ctx:
        sb, pb = memory(ctx, nc, "q")
        S = sems["q"]
        WW = DC * D
        wst = sb("wst", [P, 4 * WW])
        wh, wl = sb("wh", [P, 3 * WW], F32R), sb("wl", [P, 3 * WW], F32R)
        bq, bk = sb("bq", [P, DC]), sb("bk", [P, DC])
        brow = sb("brow", [1, 2 * D])
        bv = sb("bv", [P, D])
        cin = sb("cin", [P, TPB, D])
        xn = sb("xn", [P, TPB, D])
        st, mom = sb("st", [P, TPB, 6]), sb("mom", [P, 4, TPB])
        ve, rstd = sb("ve", [P, TPB]), sb("rstd", [P, TPB])
        xh, xl = sb("xh", [P, DC, BLK], F32R), sb("xl", [P, DC, BLK], F32R)
        ch, cl = sb("ch", [P, DC, BLK], F32R), sb("cl", [P, DC, BLK], F32R)
        vf, vr = sb("vf", [P, TPB, D]), sb("vr", [P, TPB, D])
        banks = [pb(f"bank{n}", [P, BLK]) for n in range(8)]

        def weights(n, k, m0, m):
            s = slice(n * WW + k * D + m0, n * WW + k * D + m0 + m)
            return wh[:, s], wl[:, s]

        def v_part(tile, part):
            return vs[:, bass.ds(tile * (HEADS * 3 * VW), HEADS * 3 * VW)]\
                .rearrange("p (h a v) -> p h a v", h=HEADS, a=3)[:, :, part, 0:HD]

        with nc.Block() as block:

            @block.sync
            def _(sp):
                load_split(sp, S, wst, [w["WQ"], w["WK"], w["WV"], w["WO"]])
                sp.dma_start(bq[:, :], vec["bQ"]).then_inc(S["v_in"], 16)
                sp.dma_start(bk[:, :], vec["bK"]).then_inc(S["v_in"], 16)
                sp.dma_start(brow[:, 0:D], vec["bV"]).then_inc(S["v_in"], 16)
                sp.dma_start(brow[:, D:2 * D], vec["bO"]).then_inc(S["v_in"], 16)
                with sp.Fori(0, NBLK) as i:
                    sp.wait_ge(S["cT"], 1 + DC * i)
                    sp.dma_start(cin[:, :, :], ctx_in[bass.ds(i * BLK, BLK), :]
                                 .rearrange("(t p) d -> p t d", p=P)).then_inc(S["c_in"], 16)

            @block.gpsimd
            def _(pool):
                pool.memset(vs[:, :], 0.0).then_inc(S["vzero"], 1)
                pool.wait_ge(S["vzero"], 1)
                ones = vs[:, :].rearrange("p (n a v) -> p n a v", a=3, v=VW)[:, :, 0, HD:VW]
                pool.memset(ones, 1.0).then_inc(S["vzero"], 1)
                pool.wait_ge(S["w_in"], 16 * 4)
                pool.wait_ge(S["wh"], 2)
                pool.tensor_tensor(wl[:, :], wst[:, 0:3 * WW], wh[:, :].bitcast(F32), ALU.subtract)\
                    .then_inc(S["wl"], 1)
                pool.tensor_tensor(wol[:, :], wst[:, 3 * WW:4 * WW], woh[:, :].bitcast(F32), ALU.subtract)\
                    .then_inc(S["wl"], 1)
                with pool.Fori(0, NBLK) as i:
                    pool.wait_ge(S["ve"], i + 1)
                    pool.tensor_tensor(rstd[:, :], ve[:, :], c["mhalf"][:, :], ALU.pow).then_inc(S["rstd"], 1)
                    for t in range(TPB):
                        tile = TPB * i + t
                        pool.wait_ge(S["v1"], tile + 1)
                        pool.tensor_tensor(vr[:, t, :].rearrange("p (h v) -> p h v", h=HEADS),
                                           vf[:, t, :].rearrange("p (h v) -> p h v", h=HEADS),
                                           v_part(tile, 0), ALU.subtract).then_inc(S["vr"], 1)
                        pool.wait_ge(S["v2"], tile + 1)
                        pool.tensor_tensor(v_part(tile, 2), vr[:, t, :].rearrange("p (h v) -> p h v", h=HEADS),
                                           v_part(tile, 1), ALU.subtract).then_inc(S["v3"], 1)
                pool.wait_ge(S["v3"], NT)

            @block.scalar
            def _(act):
                act.wait_ge(S["w_in"], 16 * 4)
                act.activation(wh[:, :], wst[:, 0:3 * WW], ACT.Copy).then_inc(S["wh"], 1)
                act.activation(woh[:, :], wst[:, 3 * WW:4 * WW], ACT.Copy).then_inc(S["wh"], 1)
                act.wait_ge(S["v_in"], 16 * 4)
                act.wait_ge(S["vzero"], 2)
                with act.Fori(0, NBLK) as i:
                    for k in range(DC):
                        act.wait_ge(S["xT"], 1 + DC * i + k + 1)
                        act.wait_ge(S["q"], 1 + DC * i)
                        act.activation(xh[:, k, :], banks[k][:, :], ACT.Copy).then_inc(S["xh"], 1)
                    for k in range(DC):
                        act.wait_ge(S["cT"], 1 + DC * i + k + 1)
                        act.wait_ge(S["v"], 1 + TPB * i)
                        act.activation(ch[:, k, :], banks[2 + k][:, :], ACT.Copy).then_inc(S["ch"], 1)
                    for m in range(DC):
                        act.wait_ge(S["q"], 1 + DC * i + m + 1)
                        act.activation(q_all[0][:, bass.ds(m * N + i * BLK, BLK)], banks[4 + m][:, :],
                                       ACT.Identity, bias=bq[:, m:m + 1]).then_inc(S["qh"], 1)
                    for m in range(DC):
                        act.wait_ge(S["k"], DC * i + m + 1)
                        act.activation(k_all[0][:, bass.ds(m * N + i * BLK, BLK)], banks[6 + m][:, :],
                                       ACT.Identity, bias=bk[:, m:m + 1]).then_inc(S["kh"], 1)
                    for t in range(TPB):
                        tile = TPB * i + t
                        act.wait_ge(S["vf"], 1 + tile + 1)
                        act.activation(v_part(tile, 0), vf[:, t, :].rearrange("p (h v) -> p h v", h=HEADS),
                                       ACT.Copy).then_inc(S["v1"], 1)
                    for t in range(TPB):
                        tile = TPB * i + t
                        act.wait_ge(S["vr"], 1 + tile + 1)
                        act.activation(v_part(tile, 1), vr[:, t, :].rearrange("p (h v) -> p h v", h=HEADS),
                                       ACT.Copy).then_inc(S["v2"], 1)

            @block.tensor
            def _(pe):
                pe.wait_ge(S["v_in"], 16 * 4)
                pe.matmul(banks[0][:, 0:D], c["ones"][0:1, :], brow[:, 0:D], start=True, stop=True)\
                    .then_inc(S["brows"], 1)
                pe.matmul(banks[1][:, 0:D], c["ones"][0:1, :], brow[:, D:2 * D], start=True, stop=True)\
                    .then_inc(S["brows"], 1)
                pe.wait_ge(S["wl"], 2)
                pe.wait_ge(S["bvo"], 2)
                with pe.Fori(0, NBLK) as i:
                    pe.wait_ge(S["vf"], 1 + TPB * i)
                    for k in range(DC):
                        for t in range(TPB):
                            pe.wait_ge(S["xn"], TPB * i + t + 1)
                            mm = pe.transpose(banks[k][:, t * P:(t + 1) * P], xn[:, t, k * P:(k + 1) * P],
                                              c["ident"][:, :])
                        mm.then_inc(S["xT"], 1)
                    pe.wait_ge(S["c_in"], 16 * (i + 1))
                    for k in range(DC):
                        for t in range(TPB):
                            mm = pe.transpose(banks[2 + k][:, t * P:(t + 1) * P], cin[:, t, k * P:(k + 1) * P],
                                              c["ident"][:, :])
                        mm.then_inc(S["cT"], 1)
                    pe.wait_ge(S["xh"], DC * (i + 1))
                    pe.wait_ge(S["xl"], DC * (i + 1))
                    pe.wait_ge(S["q_out"], 1 + DC * i)
                    for m in range(DC):
                        split_product(pe, banks[4 + m][:, :],
                                      [(weights(0, k, m * P, P), (xh[:, k, :], xl[:, k, :])) for k in range(DC)])\
                            .then_inc(S["q"], 1)
                    pe.wait_ge(S["ch"], DC * (i + 1))
                    pe.wait_ge(S["cl"], DC * (i + 1))
                    pe.wait_ge(S["k_out"], 1 + DC * i)
                    for m in range(DC):
                        split_product(pe, banks[6 + m][:, :],
                                      [(weights(1, k, m * P, P), (ch[:, k, :], cl[:, k, :])) for k in range(DC)])\
                            .then_inc(S["k"], 1)
                    for t in range(TPB):
                        tok = slice(t * P, (t + 1) * P)
                        split_product(pe, banks[t][:, 0:D],
                                      [((ch[:, k, tok], cl[:, k, tok]), weights(2, k, 0, D)) for k in range(DC)])\
                            .then_inc(S["v"], 1)

            @block.vector
            def _(dve):
                dve.wait_ge(S["brows"], 2)
                dve.tensor_copy(bv[:, :], banks[0][:, 0:D]).then_inc(S["bvo"], 1)
                dve.tensor_copy(bo[:, :], banks[1][:, 0:D]).then_inc(S["bvo"], 1)
                dve.wait_ge(S["bvo"], 2)
                with dve.Fori(0, NBLK) as i:
                    for t in range(TPB):
                        dve.bn_stats(st[:, t, :], x_sb[:, bass.ds((TPB * i + t) * D, D)]).then_inc(S["st"], 1)
                    dve.wait_ge(S["st"], TPB * (i + 1))
                    variance_and_mean(dve, S, st, mom, ve, i)
                    dve.wait_ge(S["rstd"], i + 1)
                    dve.wait_ge(S["xT"], 1 + DC * i)
                    for t in range(TPB):
                        dve.tensor_scalar(xn[:, t, :], x_sb[:, bass.ds((TPB * i + t) * D, D)], mom[:, 0, t:t + 1],
                                          rstd[:, t:t + 1], ALU.subtract, ALU.mult).then_inc(S["xn"], 1)
                    for k in range(DC):
                        dve.wait_ge(S["xh"], DC * i + k + 1)
                        dve.tensor_tensor(xl[:, k, :], banks[k][:, :], xh[:, k, :].bitcast(F32), ALU.subtract)\
                            .then_inc(S["xl"], 1)
                    for k in range(DC):
                        dve.wait_ge(S["ch"], DC * i + k + 1)
                        dve.tensor_tensor(cl[:, k, :], banks[2 + k][:, :], ch[:, k, :].bitcast(F32), ALU.subtract)\
                            .then_inc(S["cl"], 1)
                    for name, m, dst, bias in ([("q", m, q_all, bq) for m in range(DC)]
                                               + [("k", m, k_all, bk) for m in range(DC)]):
                        s = bass.ds(m * N + i * BLK, BLK)
                        dve.wait_ge(S[name + "h"], DC * i + m + 1)
                        dve.scalar_tensor_tensor(dst[1][:, s], banks[(4 if name == "q" else 6) + m][:, :], bias[:, m:m + 1],
                                                 dst[0][:, s].bitcast(F32), ALU.add, ALU.subtract)\
                            .then_inc(S[name + "_out"], 1)
                    for t in range(TPB):
                        dve.wait_ge(S["v"], 1 + TPB * i + t + 1)
                        dve.wait_ge(S["vr"], 1 + TPB * i)
                        dve.tensor_tensor(vf[:, t, :], banks[t][:, 0:D], bv[:, :], ALU.add).then_inc(S["vf"], 1)
                dve.wait_ge(S["k_out"], 1 + DC * NBLK)


def attention(nc, sems, c, q_all, k_all, vs, o_sb):
    UPC = 6
    U = DC * UPC
    HPC = HEADS // DC
    LAID = 16 * 2 * (1 + HPC)
    GROUPS = {1: 0, 5: 1, 7: 2, 11: 3}

    def unit(u):
        k, r = divmod(u, UPC)
        return (k, 0, 4 * r, 4) if r < 2 else (k, 1, 2 * (r - 2), 2)

    def at(b, u):
        return (b + 1, u - U) if u >= U else (b - 1, u + U) if u < 0 else (b, u)

    def ge(eng, sem, value):
        if not isinstance(value, int) or value > 0:
            eng.wait_ge(sem, value)

    def run(eng, step, before, after):
        before()
        for u in range(U):
            step(0, u, True, False)
        with eng.Fori(1, B - 1) as b:
            for u in range(U):
                step(b, u, False, False)
        for u in range(U):
            step(B - 1, u, False, True)
        after()

    with ExitStack() as ctx:
        sb, pb = memory(ctx, nc, "a")
        S = sems["a"]
        mask4 = sb("mask4", [P, 4, P], BF16)
        qh, ql = sb("qh", [P, DC, L], F32R), sb("ql", [P, DC, L], F32R)
        kxh, kxl = sb("kxh", [P, DC, HPC, L], F32R), sb("kxl", [P, DC, HPC, L], F32R)
        mx, nm = sb("mx", [P, U, 4]), sb("nm", [P, U, 4])
        pr = sb("pr", [P, 2, 4 * P])
        ph, pl = sb("ph", [P, 3, 4 * P], F16), sb("pl", [P, 3, 4 * P], F16)
        os, rc = sb("os", [P, 2, HPC, VW]), sb("rc", [P, 2, HPC])
        sbank = [pb(f"scores{n}", [P, 4 * P]) for n in range(3)]
        tbank = [pb(f"turned{n}", [P, 4 * P]) for n in range(3)]
        obank = [pb(f"out{n}", [P, 4 * P]) for n in range(2)]

        with nc.Block() as block:

            @block.gpsimd
            def _(pool):
                for m in (kxh, kxl):
                    pool.memset(m[:, :, :, :].bitcast(F32), 0.0).then_inc(S["zeros"], 1)
                for n in range(4):
                    pool.tensor_copy(mask4[:, n, :], c["mask"][:, :]).then_inc(S["mask"], 1)

            @block.sync
            def _(sp):
                def lay(b, k):
                    ge(sp, S[f"s{k}"], UPC * b)
                    for src, q, kx in ((0, qh, kxh), (1, ql, kxl)):
                        sp.dma_start(q[:, k, :].bitcast(F32), q_all[src][:, bass.ds(k * N + b * L, L)].bitcast(F32)).then_inc(S[f"laid{k}"], 16)
                        for h in range(HPC):
                            rows = slice(h * HD, (h + 1) * HD)
                            sp.dma_start(kx[rows, k, h, :].bitcast(F32), k_all[src][rows, bass.ds(k * N + b * L, L)].bitcast(F32))\
                                .then_inc(S[f"laid{k}"], 16)

                sp.wait_ge(S["zeros"], 2)
                for k in range(DC):
                    lay(0, k)
                with sp.Fori(1, B) as b:
                    for k in range(DC):
                        lay(b, k)

            @block.scalar
            def _(act):
                def exps(b, u):
                    k, q, h0, nh = unit(u)
                    n = 4 * P // nh
                    ge(act, S["nm"], U * b + u + 1)
                    ge(act, S["turned"], U * b + u - 1)
                    for j in range(nh):
                        ins = act.activation(pr[:, u % 2, j * n:(j + 1) * n], sbank[u % 3][:, j * n:(j + 1) * n],
                                             ACT.Exp, bias=nm[:, u, j:j + 1], scale=SCALE)
                    ins.then_inc(S["exp"], 1)

                def high(b, u):
                    ge(act, S["turned"], U * b + u + 1)
                    ge(act, S["pv"], U * b + u - 2)
                    act.activation(ph[:, u % 3, :], tbank[u % 3][:, :], ACT.Copy).then_inc(S["ph"], 1)

                def step(b, u, first, last):
                    exps(b, u)
                    if not (first and u < 1):
                        high(*at(b, u - 1))

                run(act, step, lambda: None, lambda: high(B - 1, U - 1))

            @block.tensor
            def _(pe):
                def scores(b, u):
                    k, q, h0, nh = unit(u)
                    if u % UPC == 0:
                        ge(pe, S[f"laid{k}"], LAID * (b + 1))
                    ge(pe, S["exp"], U * b + u - 2)
                    keys = 4 * P // nh
                    out = sbank[u % 3][:, :].rearrange("p (h k) -> p h k", h=nh)
                    tok, hs = slice(q * P, (q + 1) * P), slice(h0, h0 + nh)
                    split_product(pe, out, [((qh[:, k, tok], ql[:, k, tok]), (kxh[:, k, hs, 0:keys], kxl[:, k, hs, 0:keys]))],
                                  last=False)
                    pe.matmul(out[:, :, keys - P:keys], c["identb"][:, :], mask4[:, 0:nh, :], start=False, stop=True)\
                        .then_inc(S[f"s{k}"], 1)

                def turn(b, u):
                    ge(pe, S["exp"], U * b + u + 1)
                    ge(pe, S["pl"], U * b + u - 2)
                    for j in range(4):
                        mm = pe.transpose(tbank[u % 3][:, j * P:(j + 1) * P], pr[:, u % 2, j * P:(j + 1) * P],
                                          c["ident"][:, :])
                    mm.then_inc(S["turned"], 1)

                def weigh(b, u):
                    k, q, h0, nh = unit(u)
                    ge(pe, S["pl"], U * b + u + 1)
                    if h0 == 0:
                        ge(pe, S["o"], 4 * b + 2 * k + q - 1)
                    for j in range(nh):
                        out = obank[q][:, (h0 + j) * 3 * VW:(h0 + j + 1) * 3 * VW]
                        for t in range(q + 1):
                            v = vs[:, bass.ds(b * (2 * HEADS * 3 * VW) + (t * HEADS + k * HPC + h0 + j) * 3 * VW, 3 * VW)]
                            s = slice((j * (q + 1) + t) * P, (j * (q + 1) + t + 1) * P)
                            pe.matmul(out, ph[:, u % 3, s], v, start=t == 0, stop=False)
                            mm = pe.matmul(out, pl[:, u % 3, s], v, start=False, stop=t == q)
                    mm.then_inc(S["pv"], 1)

                def step(b, u, first, last):
                    if not (last and u >= U - 2):
                        scores(*at(b, u + 2))
                    turn(b, u)
                    if not (first and u < 2):
                        weigh(*at(b, u - 2))

                pe.wait_ge(S["mask"], 4)
                run(pe, step, lambda: [scores(0, u) for u in range(2)], lambda: [weigh(B - 1, u) for u in (U - 2, U - 1)])

            @block.vector
            def _(dve):
                def maxima(b, u):
                    k, q, h0, nh = unit(u)
                    ge(dve, S[f"s{k}"], UPC * b + u % UPC + 1)
                    dve.tensor_reduce(mx[:, u, 0:nh], sbank[u % 3][:, :].rearrange("p (h k) -> p h k", h=nh),
                                      AX.X, ALU.max).then_inc(S["mx"], 1)
                    ge(dve, S["mx"], U * b + u + 1)
                    dve.tensor_scalar(nm[:, u, 0:nh], mx[:, u, 0:nh], -SCALE, None, ALU.mult).then_inc(S["nm"], 1)

                def low(b, u):
                    ge(dve, S["ph"], U * b + u + 1)
                    ge(dve, S["pv"], U * b + u - 2)
                    dve.tensor_tensor(pl[:, u % 3, :], tbank[u % 3][:, :], ph[:, u % 3, :], ALU.subtract)\
                        .then_inc(S["pl"], 1)

                def divide(b, u):
                    if u not in GROUPS:
                        return
                    k, q = divmod(GROUPS[u], 2)
                    n = 4 * b + GROUPS[u] + 1
                    ge(dve, S["pv"], U * b + u + 1)
                    dve.tensor_reduce(os[:, q, :, :], obank[q][:, 0:HPC * 3 * VW]
                                      .rearrange("p (h a v) -> p h v a", a=3, v=VW), AX.X, ALU.add).then_inc(S["o"], 1)
                    ge(dve, S["o"], n)
                    dve.reciprocal(rc[:, q, :], os[:, q, :, HD]).then_inc(S["rc"], 1)
                    ge(dve, S["rc"], n)
                    dve.tensor_tensor(o_sb[:, bass.ds(b * (2 * D) + q * D + k * P, P)].rearrange("p (h v) -> p h v", h=HPC),
                                      os[:, q, :, 0:HD], rc[:, q, :].unsqueeze(2).to_broadcast([P, HPC, HD]),
                                      ALU.mult).then_inc(S["on"], 1)

                def step(b, u, first, last):
                    maxima(b, u)
                    if not (first and u < 2):
                        low(*at(b, u - 2))
                    if not (first and u < 3):
                        divide(*at(b, u - 3))

                def after():
                    for u in (U - 2, U - 1):
                        low(B - 1, u)
                    for u in (U - 3, U - 2, U - 1):
                        divide(B - 1, u)
                    dve.wait_ge(S["on"], 4 * B)

                run(dve, step, lambda: None, after)


def output_and_router(nc, sems, c, x_sb, o_sb, x3, lg, woh, wol, bo, router_w):
    with ExitStack() as ctx:
        sb, pb = memory(ctx, nc, "w")
        S = sems["w"]
        rw = sb("rw", [P, DC, E])
        oh, ol = sb("oh", [P, DC, BLK], F32R), sb("ol", [P, DC, BLK], F32R)
        t1, t2 = sb("t1", [P, TPB, D]), sb("t2", [P, TPB, D])
        st, mom = sb("st", [P, TPB, 6]), sb("mom", [P, 4, TPB])
        ve, rstd = sb("ve", [P, TPB]), sb("rstd", [P, TPB])
        xt = sb("xt", [P, DC, BLK])
        ob, xb = [pb(f"ob{n}", [P, BLK]) for n in range(2)], [pb(f"xb{n}", [P, BLK]) for n in range(2)]
        yb = [pb(f"yb{n}", [P, BLK]) for n in range(3)]
        lb = pb("lb", [P, BLK])

        def tile(m, i, t):
            return m[:, bass.ds((TPB * i + t) * D, D)]

        with nc.Block() as block:

            @block.sync
            def _(sp):
                sp.dma_start(rw[:, :, :], router_w.rearrange("(k p) e -> p k e", p=P)).then_inc(S["rw"], 16)

            @block.gpsimd
            def _(pool):
                with pool.Fori(0, NBLK) as i:
                    pool.wait_ge(S["ve"], i + 1)
                    pool.tensor_tensor(rstd[:, :], ve[:, :], c["mhalf"][:, :], ALU.pow).then_inc(S["rstd"], 1)

            @block.scalar
            def _(act):
                with act.Fori(0, NBLK) as i:
                    for k in range(DC):
                        act.wait_ge(S["oT"], DC * i + k + 1)
                        act.wait_ge(S["y"], 1 + TPB * i)
                        act.activation(oh[:, k, :], ob[k][:, :], ACT.Copy).then_inc(S["oh"], 1)
                    for k in range(DC):
                        act.wait_ge(S["xT"], 1 + DC * i + k + 1)
                        act.wait_ge(S["lg"], 1 + i)
                        act.activation(xt[:, k, :], xb[k][:, :], ACT.Copy).then_inc(S["xt"], 1)
                    for t in range(TPB):
                        act.activation(tile(x_sb, i, t), t2[:, t, :], ACT.Copy).then_inc(S["x2_out"], 1)
                        act.activation(tile(x3, i, t), t1[:, t, :], ACT.Copy).then_inc(S["x3_out"], 1)
                act.wait_ge(S["x2_out"], 1 + NT)
                act.wait_ge(S["x3_out"], 1 + NT)

            @block.tensor
            def _(pe):
                pe.wait_ge(S["rw"], 16)
                with pe.Fori(0, NBLK) as i:
                    pe.wait_ge(S["ol"], 1 + DC * i)
                    for k in range(DC):
                        for t in range(TPB):
                            pe.wait_ge(S["o_tile"], TPB * i + t + 1)
                            mm = pe.transpose(ob[k][:, t * P:(t + 1) * P], t1[:, t, k * P:(k + 1) * P], c["ident"][:, :])
                        mm.then_inc(S["oT"], 1)
                    pe.wait_ge(S["oh"], DC * (i + 1))
                    pe.wait_ge(S["ol"], 1 + DC * (i + 1))
                    for t in range(TPB):
                        pe.wait_ge(S["ya"], 1 + TPB * i + max(t - 2, 0))
                        tok = slice(t * P, (t + 1) * P)
                        split_product(pe, yb[t % 3][:, 0:D],
                                      [((oh[:, k, tok], ol[:, k, tok]),
                                        (woh[:, k * D:(k + 1) * D], wol[:, k * D:(k + 1) * D])) for k in range(DC)])\
                            .then_inc(S["y"], 1)
                    pe.wait_ge(S["x3"], TPB * (i + 1))
                    pe.wait_ge(S["xt"], 1 + DC * i)
                    for k in range(DC):
                        for t in range(TPB):
                            mm = pe.transpose(xb[k][:, t * P:(t + 1) * P], t1[:, t, k * P:(k + 1) * P], c["ident"][:, :])
                        mm.then_inc(S["xT"], 1)
                    pe.wait_ge(S["xt"], 1 + DC * (i + 1))
                    pe.wait_ge(S["lg_out"], 1 + i)
                    for t in range(TPB):
                        for k in range(DC):
                            mm = pe.matmul(lb[:, t * E:(t + 1) * E], xt[:, k, t * P:(t + 1) * P], rw[:, k, :],
                                           start=k == 0, stop=k == DC - 1)
                    mm.then_inc(S["lg"], 1)

            @block.vector
            def _(dve):
                with dve.Fori(0, NBLK) as i:
                    for t in range(TPB):
                        dve.wait_ge(S["xT"], 1 + DC * i)
                        dve.wait_ge(S["x3_out"], 1 + TPB * i)
                        dve.tensor_copy(t1[:, t, :], tile(o_sb, i, t)).then_inc(S["o_tile"], 1)
                    for k in range(DC):
                        dve.wait_ge(S["oh"], DC * i + k + 1)
                        dve.tensor_tensor(ol[:, k, :], ob[k][:, :], oh[:, k, :].bitcast(F32), ALU.subtract)\
                            .then_inc(S["ol"], 1)
                    for t in range(TPB):
                        n = TPB * i + t + 1
                        dve.wait_ge(S["y"], 1 + n)
                        dve.tensor_tensor(t1[:, t, :], yb[t % 3][:, 0:D], bo[:, :], ALU.add).then_inc(S["ya"], 1)
                        dve.wait_ge(S["ya"], 1 + n)
                        dve.wait_ge(S["x2_out"], 1 + TPB * i)
                        dve.tensor_tensor(t2[:, t, :], t1[:, t, :], tile(x_sb, i, t), ALU.add).then_inc(S["x2"], 1)
                        dve.wait_ge(S["x2"], 1 + n)
                        dve.bn_stats(st[:, t, :], t2[:, t, :]).then_inc(S["st"], 1)
                    dve.wait_ge(S["st"], TPB * (i + 1))
                    variance_and_mean(dve, S, st, mom, ve, i)
                    dve.wait_ge(S["rstd"], i + 1)
                    for t in range(TPB):
                        dve.tensor_scalar(t1[:, t, :], t2[:, t, :], mom[:, 0, t:t + 1], rstd[:, t:t + 1],
                                          ALU.subtract, ALU.mult).then_inc(S["x3"], 1)
                    dve.wait_ge(S["lg"], 1 + i + 1)
                    dve.tensor_copy(lg[:, bass.ds(i * (TPB * E), TPB * E)], lb[:, 0:TPB * E]).then_inc(S["lg_out"], 1)
                dve.wait_ge(S["lg_out"], 1 + NBLK)


def route(nc, sems, c, x3, lg, cw, gi, zero, disp):
    with ExitStack() as ctx:
        sb, pb = memory(ctx, nc, "r")
        S = sems["r"]
        m8, i8 = sb("m8", [P, NT, 8]), sb("i8", [P, NT, 8], U32)
        ef = sb("ef", [P, K, NT])
        oh = sb("oh", [P, K, NT, E])
        both, incl, excl = sb("both", [P, NT, E]), sb("incl", [P, NT, E]), sb("excl", [P, NT, E])
        rk, tmp = sb("rk", [P, NT, E]), sb("tmp", [P, K, NT, E])
        rank, keep, base = sb("rank", [P, K, NT]), sb("keep", [P, K, NT]), sb("base", [P, K, NT])
        sf, gf, far = sb("sf", [P, K, NT]), sb("gf", [P, K, NT]), sb("far", [P, K, NT])
        si = sb("si", [P, K, NT], U32)
        d, ex, one = sb("d", [P, NT]), sb("ex", [P, NT]), sb("one", [P, NT])
        wr = sb("wr", [P, K, NT])
        rb = pb("rb", [P, NT * E])

        with nc.Block() as block:

            @block.sync
            def _(sp):
                for e in range(E):
                    sp.dma_start(disp[e * SLOTS:(e + 1) * SLOTS, :].rearrange("(p t) d -> p t d", t=ST),
                                 zero[:, :, :]).then_inc(S["zeroed"], 16)

            @block.scalar
            def _(act):
                act.wait_ge(S["d"], 1)
                act.activation(ex[:, :], d[:, :], ACT.Exp).then_inc(S["ex"], 1)

            @block.tensor
            def _(pe):
                pe.wait_ge(S["excl"], 1)
                pe.matmul(rb[:, :], c["before"][:, :], both[:, :, :].rearrange("p t e -> p (t e)"), start=True, stop=False)
                pe.matmul(rb[:, :], c["ones"][:, :], excl[:, :, :].rearrange("p t e -> p (t e)"), start=False, stop=True)\
                    .then_inc(S["rb"], 1)

            @block.gpsimd
            def _(pool):
                pool.wait_ge(S["zeroed"], 16 * E)
                pool.wait_ge(S["si"], 1)
                for t in range(NT):
                    for k in range(K):
                        pool.indirect_dma_start(
                            out=disp, out_offset=bass.IndirectOffsetOnAxis(ap=si[:, k, t:t + 1], axis=0),
                            in_=x3[:, t * D:(t + 1) * D], in_offset=None,
                            bounds_check=E * SLOTS - 1, oob_is_err=False).then_inc(S["sent"], 16)
                pool.wait_ge(S["sent"], 16 * K * NT)

            @block.vector
            def _(dve):
                n = [0]

                def chain(ins):
                    n[0] += 1
                    ins.then_inc(S["step"], 1)
                    dve.wait_ge(S["step"], n[0])

                for t in range(NT):
                    dve.max(m8[:, t, :], lg[:, t * E:(t + 1) * E]).then_inc(S["m8"], 1)
                for t in range(NT):
                    dve.wait_ge(S["m8"], t + 1)
                    dve.max_index(i8[:, t, :], m8[:, t, :], lg[:, t * E:(t + 1) * E]).then_inc(S["i8"], 1)
                dve.tensor_tensor(d[:, :], m8[:, :, 1], m8[:, :, 0], ALU.subtract).then_inc(S["d"], 1)
                dve.wait_ge(S["i8"], NT)
                for k in range(K):
                    chain(dve.tensor_copy(ef[:, k, :], i8[:, :, k]))
                    chain(dve.tensor_tensor(oh[:, k, :, :], ef[:, k, :].unsqueeze(2).to_broadcast([P, NT, E]),
                                            c["iota"][:, :].unsqueeze(1).to_broadcast([P, NT, E]), ALU.is_equal))
                chain(dve.tensor_tensor(both[:, :, :], oh[:, 0, :, :], oh[:, 1, :, :], ALU.add))
                for e in range(E):
                    chain(dve.tensor_tensor_scan(incl[:, :, e], both[:, :, e], both[:, :, e], 0.0, ALU.add, ALU.bypass))
                dve.tensor_tensor(excl[:, :, :], incl[:, :, :], both[:, :, :], ALU.subtract).then_inc(S["excl"], 1)
                dve.wait_ge(S["ex"], 1)
                chain(dve.tensor_scalar(one[:, :], ex[:, :], 1.0, None, ALU.add))
                chain(dve.reciprocal(wr[:, 0, :], one[:, :]))
                chain(dve.tensor_tensor(wr[:, 1, :], ex[:, :], wr[:, 0, :], ALU.mult))
                dve.wait_ge(S["rb"], 1)
                chain(dve.tensor_copy(rk[:, :, :].rearrange("p t e -> p (t e)"), rb[:, :]))
                for k in range(K):
                    chain(dve.tensor_tensor(tmp[:, k, :, :], rk[:, :, :], oh[:, k, :, :], ALU.mult))
                    chain(dve.tensor_reduce(rank[:, k, :], tmp[:, k, :, :], AX.X, ALU.add))
                chain(dve.tensor_scalar(keep[:, :, :], rank[:, :, :], float(CAP), None, ALU.is_lt))
                chain(dve.tensor_scalar(base[:, :, :], ef[:, :, :], float(SLOTS), None, ALU.mult))
                chain(dve.scalar_tensor_tensor(gf[:, :, :], rank[:, :, :], float(CAP - 1), base[:, :, :], ALU.min, ALU.add))
                chain(dve.tensor_scalar(far[:, :, :], keep[:, :, :], -float(FAR), float(FAR), ALU.mult, ALU.add))
                chain(dve.tensor_tensor(sf[:, :, :], far[:, :, :], gf[:, :, :], ALU.add))
                dve.tensor_copy(si[:, :, :], sf[:, :, :]).then_inc(S["si"], 1)
                chain(dve.tensor_copy(gi[:, :, :], gf[:, :, :]))
                chain(dve.tensor_tensor(cw[:, :, :], wr[:, :, :], keep[:, :, :], ALU.mult))


def experts(nc, sems, c, disp, ybuf, w1, w2):
    W1 = DC * FF
    W2 = FC * D
    VB = 4
    PIECE = W2 // 4
    with ExitStack() as ctx:
        sb, pb = memory(ctx, nc, "f")
        S = sems["f"]
        s1, s2 = sb("s1", [P, W1]), sb("s2", [P, W2])
        w1h, w1l = sb("w1h", [P, W1], F32R), sb("w1l", [P, W1], F32R)
        w2h, w2l = sb("w2h", [P, W2], F32R), sb("w2l", [P, W2], F32R)
        rows = sb("rows", [SP_, ST, D])
        xh, xl = sb("xh", [P, DC, SLOTS], F32R), sb("xl", [P, DC, SLOTS], F32R)
        th, v = sb("th", [P, 2, HALF]), sb("v", [P, VB, HALF])
        hh, hl = sb("hh", [P, FC, SLOTS], F32R), sb("hl", [P, FC, SLOTS], F32R)
        y = sb("y", [SP_, ST, D])
        tb = [pb(f"tb{n}", [P, 512]) for n in range(2)]
        hb = [pb(f"hb{n}", [P, 512]) for n in range(3)]
        yb = [pb(f"yb{n}", [P, 512]) for n in range(3)]
        HU = 2 * FC
        TU = 2 * DC

        def turn_unit(n):
            f, k = divmod(n, DC)
            return k, f, slice(f * HALF, (f + 1) * HALF)

        with nc.Block() as block:

            @block.sync
            def _(sp):
                with sp.Fori(0, E) as e:
                    sp.wait_ge(S["T"], 1 + TU * e)
                    sp.dma_start(rows[:, :, :], disp[bass.ds(e * SLOTS, SLOTS), :].rearrange("(p t) d -> p t d", t=ST))\
                        .then_inc(S["rows"], 16)
                    sp.wait_ge(S["w1l"], 1 + e)
                    sp.dma_start(s1[:, :].rearrange("p (k f) -> p k f", k=DC),
                                 w1[bass.ds(e * D, D), :].rearrange("(k p) f -> p k f", p=P)).then_inc(S["s1"], 16)
                    sp.wait_ge(S["w2l"], 1 + 4 * e)
                    sp.dma_start(s2[:, :].rearrange("p (k d) -> p k d", k=FC),
                                 w2[bass.ds(e * FF, FF), :].rearrange("(k p) d -> p k d", p=P)).then_inc(S["s2"], 16)

            @block.gpsimd
            def _(pool):
                def split_w1(e):
                    pool.wait_ge(S["w1h"], e + 1)
                    pool.tensor_tensor(w1l[:, :], s1[:, :], w1h[:, :].bitcast(F32), ALU.subtract).then_inc(S["w1l"], 1)

                def hidden(e):
                    for u in range(1, HU, 2):
                        f, s = u // 2, slice(HALF, SLOTS)
                        pool.wait_ge(S["hh"], HU * e + u + 1)
                        if u == 1:
                            pool.wait_ge(S["y"], 1 + ST * e)
                        pool.tensor_tensor(hl[:, f, s], v[:, u % VB, :], hh[:, f, s].bitcast(F32), ALU.subtract)\
                            .then_inc(S["hl_odd"], 1)
                        if 3 <= u < 11:
                            n = (u - 3) // 2
                            p = slice(n * PIECE, (n + 1) * PIECE)
                            pool.wait_ge(S["w2h"], 4 * e + n + 1)
                            pool.tensor_tensor(w2l[:, p], s2[:, p], w2h[:, p].bitcast(F32), ALU.subtract)\
                                .then_inc(S["w2l"], 1)

                split_w1(0)
                with pool.Fori(0, E - 1) as e:
                    hidden(e)
                    split_w1(e + 1)
                hidden(E - 1)

            @block.scalar
            def _(act):
                def split_w1(e):
                    act.wait_ge(S["s1"], 16 * (e + 1))
                    act.wait_ge(S["h"], 1 + HU * e)
                    act.activation(w1h[:, :], s1[:, :], ACT.Copy).then_inc(S["w1h"], 1)

                def turned(e, n):
                    k, f, s = turn_unit(n)
                    act.wait_ge(S["T"], 1 + TU * e + n + 1)
                    act.activation(xh[:, k, s], tb[n % 2][:, 0:HALF], ACT.Copy).then_inc(S["xh"], 1)

                def hidden(e):
                    for u in range(HU + 2):
                        if u < HU:
                            act.wait_ge(S["h"], 1 + HU * e + u + 1)
                            act.wait_ge(S["v"], 1 + HU * e + max(u - 1, 0))
                            act.activation(th[:, u % 2, :], hb[u % 3][:, 0:HALF], ACT.Tanh, scale=0.5).then_inc(S["th"], 1)
                        if u >= 2:
                            f, s = divmod(u - 2, 2)
                            if u == 2:
                                act.wait_ge(S["y"], 1 + ST * e)
                            act.wait_ge(S["v"], 1 + HU * e + u - 1)
                            act.activation(hh[:, f, s * HALF:(s + 1) * HALF], v[:, (u - 2) % VB, :], ACT.Copy)\
                                .then_inc(S["hh"], 1)

                def result(e, t):
                    act.wait_ge(S["y"], 1 + ST * e + t + 1)
                    if t == 0:
                        act.wait_ge(S["stored"], 1 + 16 * e)
                    act.activation(y[:, t, :], yb[t % 3][0:SP_, 0:D], ACT.Copy, scale=0.5).then_inc(S["y_out"], 1)

                def store(e):
                    act.wait_ge(S["y_out"], 1 + ST * (e + 1))
                    act.dma_start(ybuf[bass.ds(e * SLOTS, SLOTS), :].rearrange("(p t) d -> p t d", t=ST), y[:, :, :])\
                        .then_inc(S["stored"], 16)

                split_w1(0)
                for n in range(TU):
                    turned(0, n)
                with act.Fori(0, E - 1) as e:
                    hidden(e)
                    split_w1(e + 1)
                    turned(e + 1, 0)
                    turned(e + 1, 1)
                    result(e, 0)
                    turned(e + 1, 2)
                    turned(e + 1, 3)
                    for t in range(1, ST):
                        result(e, t)
                    store(e)
                hidden(E - 1)
                for t in range(ST):
                    result(E - 1, t)
                store(E - 1)
                act.wait_ge(S["stored"], 1 + 16 * E)

            @block.tensor
            def _(pe):
                def turn(e, n):
                    k, f, _ = turn_unit(n)
                    if n == 0:
                        pe.wait_ge(S["rows"], 16 * (e + 1))
                    pe.wait_ge(S["xl"], 1 + TU * e + max(n - 1, 0))
                    for t in range(3):
                        mm = pe.transpose(tb[n % 2][:, t * SP_:(t + 1) * SP_], rows[:, 3 * f + t, k * P:(k + 1) * P],
                                          c["ident"][0:SP_, 0:SP_])
                    mm.then_inc(S["T"], 1)

                def hidden(e):
                    pe.wait_ge(S["xh"], TU * (e + 1))
                    pe.wait_ge(S["xl"], 1 + TU * (e + 1))
                    pe.wait_ge(S["w1l"], 1 + e + 1)
                    for u in range(HU):
                        f, s = divmod(u, 2)
                        pe.wait_ge(S["v"], 1 + HU * e + max(u - 2, 0))
                        split_product(pe, hb[u % 3][:, 0:HALF],
                                      [((w1h[:, k * FF + f * P:k * FF + (f + 1) * P], w1l[:, k * FF + f * P:k * FF + (f + 1) * P]),
                                        (xh[:, k, s * HALF:(s + 1) * HALF], xl[:, k, s * HALF:(s + 1) * HALF]))
                                       for k in range(DC)]).then_inc(S["h"], 1)

                def result(e, t):
                    if t == 0:
                        pe.wait_ge(S["w2l"], 1 + 4 * (e + 1))
                    pe.wait_ge(S["y_out"], 1 + ST * e + max(t - 2, 0))
                    s = slice(t * SP_, (t + 1) * SP_)
                    for f in range(FC):
                        if t == 0:
                            pe.wait_ge(S["hl"], 1 + FC * e + f + 1)
                            pe.wait_ge(S["hl_odd"], 1 + FC * e + f + 1)
                        mm = split_product(pe, yb[t % 3][0:SP_, 0:D],
                                           [((hh[:, f, s], hl[:, f, s]), (w2h[:, f * D:(f + 1) * D], w2l[:, f * D:(f + 1) * D]))],
                                           first=f == 0, last=f == FC - 1)
                    mm.then_inc(S["y"], 1)

                for n in range(TU):
                    turn(0, n)
                with pe.Fori(0, E - 1) as e:
                    hidden(e)
                    turn(e + 1, 0)
                    turn(e + 1, 1)
                    result(e, 0)
                    turn(e + 1, 2)
                    turn(e + 1, 3)
                    for t in range(1, ST):
                        result(e, t)
                hidden(E - 1)
                for t in range(ST):
                    result(E - 1, t)

            @block.vector
            def _(dve):
                def turned(e, n):
                    k, f, s = turn_unit(n)
                    dve.wait_ge(S["xh"], TU * e + n + 1)
                    dve.tensor_tensor(xl[:, k, s], tb[n % 2][:, 0:HALF], xh[:, k, s].bitcast(F32), ALU.subtract)\
                        .then_inc(S["xl"], 1)

                def hidden(e):
                    for u in range(HU + 3):
                        if u < HU:
                            dve.wait_ge(S["th"], HU * e + u + 1)
                            dve.wait_ge(S["hl_odd"], 1 + FC * e + max((u - 3) // 2, 0))
                            dve.wait_ge(S["hl"], 1 + FC * e + max((u - 2) // 2, 0))
                            dve.scalar_tensor_tensor(v[:, u % VB, :], th[:, u % 2, :], 1.0, hb[u % 3][:, 0:HALF],
                                                     ALU.add, ALU.mult).then_inc(S["v"], 1)
                        if u >= 3 and (u - 3) % 2 == 0:
                            f, s = (u - 3) // 2, slice(0, HALF)
                            dve.wait_ge(S["hh"], HU * e + u - 2)
                            dve.tensor_tensor(hl[:, f, s], v[:, (u - 3) % VB, :], hh[:, f, s].bitcast(F32), ALU.subtract)\
                                .then_inc(S["hl"], 1)
                        if u in (2, 4, 6, 8):
                            n = u // 2 - 1
                            p = slice(n * PIECE, (n + 1) * PIECE)
                            if n == 0:
                                dve.wait_ge(S["s2"], 16 * (e + 1))
                                dve.wait_ge(S["y"], 1 + ST * e)
                            dve.tensor_copy(w2h[:, p], s2[:, p]).then_inc(S["w2h"], 1)

                for n in range(TU):
                    turned(0, n)
                with dve.Fori(0, E - 1) as e:
                    hidden(e)
                    for n in range(TU):
                        turned(e + 1, n)
                hidden(E - 1)


def combine(nc, sems, x_sb, x3, cw, gi, ybuf, out):
    with ExitStack() as ctx:
        sb, _ = memory(ctx, nc, "o")
        S = sems["o"]
        got = sb("got", [P, NT * K * D])
        acc = sb("acc", [P, NT * D])
        with nc.Block() as block:

            @block.gpsimd
            def _(pool):
                for t in range(NT):
                    for k in range(K):
                        at = (t * K + k) * D
                        pool.indirect_dma_start(
                            out=got[:, at:at + D], out_offset=None, in_=ybuf,
                            in_offset=bass.IndirectOffsetOnAxis(ap=gi[:, k, t:t + 1], axis=0),
                            bounds_check=E * SLOTS - 1, oob_is_err=False).then_inc(S[f"got{t // TPB}"], 16)

            @block.vector
            def _(dve):
                for t in range(NT):
                    s, g = slice(t * D, (t + 1) * D), t * K * D
                    dve.wait_ge(S[f"got{t // TPB}"], 16 * K * TPB)
                    dve.scalar_tensor_tensor(acc[:, s], got[:, g:g + D], cw[:, 0, t:t + 1], x3[:, s], ALU.mult, ALU.add)\
                        .then_inc(S["a"], 1)
                    dve.wait_ge(S["a"], 3 * t + 1)
                    dve.scalar_tensor_tensor(acc[:, s], got[:, g + D:g + 2 * D], cw[:, 1, t:t + 1], acc[:, s],
                                             ALU.mult, ALU.add).then_inc(S["a"], 1)
                    dve.wait_ge(S["a"], 3 * t + 2)
                    dve.tensor_tensor(acc[:, s], acc[:, s], x_sb[:, s], ALU.add).then_inc(S["a"], 1)

            @block.sync
            def _(sp):
                for i in range(NBLK):
                    sp.wait_ge(S["a"], 3 * TPB * (i + 1))
                    sp.dma_start(out[i * BLK:(i + 1) * BLK, :].rearrange("(t p) d -> p t d", p=P),
                                 acc[:, i * TPB * D:(i + 1) * TPB * D].rearrange("p (t d) -> p t d", d=D))\
                        .then_inc(S["stored"], 16)
                sp.wait_ge(S["stored"], 16 * NBLK)


def build(nc, a, out, phases="MQWFC"):
    with ExitStack() as ctx:
        sems = {phase: Sems(ctx, nc, phase) for phase in "cmqawrfo"}
        sb, _ = memory(ctx, nc, "g")
        x_sb = sb("x", [P, NT * D])
        c = constants(nc, ctx, sems)
        w = {n: a["L0_attn_" + n] for n in MIX}
        vec = {n: a["L0_attn_" + n] for n in ("conv_w", "conv_b", "dl_b", "A_b", "B_b", "C_b", "D_b")}
        mixer(nc, sems, c, x_sb, a["x"], w, vec)
        if "Q" in phases:
            woh, wol = sb("woh", [P, DC * D], F32R), sb("wol", [P, DC * D], F32R)
            bo, o_sb = sb("bo", [P, D]), sb("o", [P, NT * D])
            with ExitStack() as qkv:
                sb3, _ = memory(qkv, nc, "i")
                q_all = [sb3(f"q{n}", [P, DC * N], F32R) for n in range(2)]
                k_all = [sb3(f"k{n}", [P, DC * N], F32R) for n in range(2)]
                vs = sb3("vs", [P, NT * HEADS * 3 * VW], BF16)
                wx = {n: a["L0_xattn_" + n] for n in ("WQ", "WK", "WV", "WO", "bQ", "bK", "bV", "bO")}
                projections(nc, sems, c, x_sb, a["ctx_1024"], wx, wx, q_all, k_all, vs, woh, wol, bo)
                attention(nc, sems, c, q_all, k_all, vs, o_sb)
            x3, lg = sb("x3", [P, NT * D]), sb("lg", [P, NT * E])
            output_and_router(nc, sems, c, x_sb, o_sb, x3, lg, woh, wol, bo, a["L0_ffn_router_w"])
        if "F" in phases:
            cw, gi = sb("cw", [P, K, NT]), sb("gi", [P, K, NT], U32)
            disp = nc.dram_tensor("disp", (E * SLOTS, D), F32).ap()
            ybuf = nc.dram_tensor("ybuf", (E * SLOTS, D), F32).ap()
            route(nc, sems, c, x3, lg, cw, gi, c["zero"], disp)
            experts(nc, sems, c, disp, ybuf, a["L0_ffn_w1"], a["L0_ffn_w2"])
            combine(nc, sems, x_sb, x3, cw, gi, ybuf, out)
            return
        done = ctx.enter_context(nc.semaphore("done"))
        with nc.Block() as block:
            @block.sync
            def _(sp):
                sp.dma_start(out.rearrange("(t p) d -> p t d", p=P),
                             x_sb[:, :].rearrange("p (t d) -> p t d", d=D)).then_inc(done, 16)
                sp.wait_ge(done, 16)


def layout(inputs):
    import numpy as np
    out = {}
    for name, v in inputs.items():
        v = np.asarray(v)
        short = name.replace("L0_attn_", "")
        if name.startswith("L0_attn_") and short in MIX or name == "L0_ffn_router_w":
            v = v.T
        elif short == "conv_w":
            v = v.reshape(D, 3)
        elif name in ("L0_xattn_bV", "L0_xattn_bO"):
            v = v.reshape(1, D)
        elif v.ndim == 1:
            v = v.reshape(-1, P).T
        elif v.ndim == 3:
            v = v.reshape(-1, v.shape[-1])
        out[name] = np.ascontiguousarray(v)
    return out


_OUT = (B, L, D)


def kernel(**inputs):
    import numpy as _np
    import concourse.bacc as _bacc
    from concourse import mybir as _mybir
    from concourse.bass_utils import run_bass_kernel_spmd as _run

    nc = _bacc.Bacc("TRN2", target_bir_lowering=False, num_devices=1)
    arrays = {f"in_{n}": v for n, v in layout(inputs).items()}
    args = {n[3:]: nc.dram_tensor(n, v.shape, _mybir.dt.from_np(v.dtype), kind="ExternalInput").ap()
            for n, v in arrays.items()}
    out = nc.dram_tensor("out", (N, D), F32, kind="ExternalOutput").ap()
    build(nc, args, out)
    r = _run(nc, [arrays], core_ids=[0])
    return _np.asarray(r.results[0]["out"]).reshape(_OUT)
```
